# Optimizing a Trainium2 kernel written in Bass

```python
import numpy as np
import jax
import jax.numpy as jnp

def _softmax(x, axis=-1):
    return jax.nn.softmax(x, axis=axis)

def _gelu(x):
    return jax.nn.gelu(x, approximate=True)

def _silu(x):
    return jax.nn.silu(x)

def _sigmoid(x):
    return jax.nn.sigmoid(x)

def _layernorm(x, axis=-1, eps=1e-05):
    m = jnp.mean(x, axis=axis, keepdims=True)
    v = jnp.var(x, axis=axis, keepdims=True)
    return (x - m) / jnp.sqrt(v + eps)

def _scatter_add(tgt, idx, src, axis=0):
    return tgt.at[idx].add(src)

def _segment_sum(src, seg, n):
    return jax.ops.segment_sum(src, seg, n)
kernel_name = 'mk_dlrm_tower_d1_rec_r8_902fcd'

def setup_inputs(seed: int=0):
    np.random.seed(seed)
    _w = jnp.asarray

    def _rec_inputs():
        import jax
        import jax.numpy as jnp
        _tk = jax.random.key(seed)
        dense_ctx = jax.random.normal(jax.random.fold_in(_tk, 190), (1024, 16), jnp.float32)
        ids = jnp.stack([jax.random.randint(jax.random.fold_in(_tk, 200 + f), (1024,), 0, v, jnp.int32) for f, v in enumerate([125000, 125000, 125000, 1250, 1000, 1000, 1250, 12500, 1250, 125000, 1000, 125000, 1000, 12500, 1250, 12500, 12500, 1250, 1250, 125000, 125000, 12500, 12500, 1250, 1000, 1000, 12500, 1250, 1250, 1000, 1000, 1250])], axis=1)
        tbl_0 = 0.05 * jax.random.normal(jax.random.fold_in(_tk, 500 + 0), (125000, 32), jnp.float32)
        tbl_1 = 0.05 * jax.random.normal(jax.random.fold_in(_tk, 500 + 1), (125000, 32), jnp.float32)
        tbl_2 = 0.05 * jax.random.normal(jax.random.fold_in(_tk, 500 + 2), (125000, 32), jnp.float32)
        tbl_3 = 0.05 * jax.random.normal(jax.random.fold_in(_tk, 500 + 3), (1250, 32), jnp.float32)
        tbl_4 = 0.05 * jax.random.normal(jax.random.fold_in(_tk, 500 + 4), (1000, 32), jnp.float32)
        tbl_5 = 0.05 * jax.random.normal(jax.random.fold_in(_tk, 500 + 5), (1000, 32), jnp.float32)
        tbl_6 = 0.05 * jax.random.normal(jax.random.fold_in(_tk, 500 + 6), (1250, 32), jnp.float32)
        tbl_7 = 0.05 * jax.random.normal(jax.random.fold_in(_tk, 500 + 7), (12500, 32), jnp.float32)
        tbl_8 = 0.05 * jax.random.normal(jax.random.fold_in(_tk, 500 + 8), (1250, 32), jnp.float32)
        tbl_9 = 0.05 * jax.random.normal(jax.random.fold_in(_tk, 500 + 9), (125000, 32), jnp.float32)
        tbl_10 = 0.05 * jax.random.normal(jax.random.fold_in(_tk, 500 + 10), (1000, 32), jnp.float32)
        tbl_11 = 0.05 * jax.random.normal(jax.random.fold_in(_tk, 500 + 11), (125000, 32), jnp.float32)
        tbl_12 = 0.05 * jax.random.normal(jax.random.fold_in(_tk, 500 + 12), (1000, 32), jnp.float32)
        tbl_13 = 0.05 * jax.random.normal(jax.random.fold_in(_tk, 500 + 13), (12500, 32), jnp.float32)
        tbl_14 = 0.05 * jax.random.normal(jax.random.fold_in(_tk, 500 + 14), (1250, 32), jnp.float32)
        tbl_15 = 0.05 * jax.random.normal(jax.random.fold_in(_tk, 500 + 15), (12500, 32), jnp.float32)
        tbl_16 = 0.05 * jax.random.normal(jax.random.fold_in(_tk, 500 + 16), (12500, 32), jnp.float32)
        tbl_17 = 0.05 * jax.random.normal(jax.random.fold_in(_tk, 500 + 17), (1250, 32), jnp.float32)
        tbl_18 = 0.05 * jax.random.normal(jax.random.fold_in(_tk, 500 + 18), (1250, 32), jnp.float32)
        tbl_19 = 0.05 * jax.random.normal(jax.random.fold_in(_tk, 500 + 19), (125000, 32), jnp.float32)
        tbl_20 = 0.05 * jax.random.normal(jax.random.fold_in(_tk, 500 + 20), (125000, 32), jnp.float32)
        tbl_21 = 0.05 * jax.random.normal(jax.random.fold_in(_tk, 500 + 21), (12500, 32), jnp.float32)
        tbl_22 = 0.05 * jax.random.normal(jax.random.fold_in(_tk, 500 + 22), (12500, 32), jnp.float32)
        tbl_23 = 0.05 * jax.random.normal(jax.random.fold_in(_tk, 500 + 23), (1250, 32), jnp.float32)
        tbl_24 = 0.05 * jax.random.normal(jax.random.fold_in(_tk, 500 + 24), (1000, 32), jnp.float32)
        tbl_25 = 0.05 * jax.random.normal(jax.random.fold_in(_tk, 500 + 25), (1000, 32), jnp.float32)
        tbl_26 = 0.05 * jax.random.normal(jax.random.fold_in(_tk, 500 + 26), (12500, 32), jnp.float32)
        tbl_27 = 0.05 * jax.random.normal(jax.random.fold_in(_tk, 500 + 27), (1250, 32), jnp.float32)
        tbl_28 = 0.05 * jax.random.normal(jax.random.fold_in(_tk, 500 + 28), (1250, 32), jnp.float32)
        tbl_29 = 0.05 * jax.random.normal(jax.random.fold_in(_tk, 500 + 29), (1000, 32), jnp.float32)
        tbl_30 = 0.05 * jax.random.normal(jax.random.fold_in(_tk, 500 + 30), (1000, 32), jnp.float32)
        tbl_31 = 0.05 * jax.random.normal(jax.random.fold_in(_tk, 500 + 31), (1250, 32), jnp.float32)
        _rk = jax.random.fold_in(_tk, 7)
        W_top1 = 0.0606339 * jax.random.normal(jax.random.fold_in(_tk, 801), (272, 512), jnp.float32)
        W_top2 = 0.0441942 * jax.random.normal(jax.random.fold_in(_tk, 802), (512, 256), jnp.float32)
        W_top3 = 0.0625 * jax.random.normal(jax.random.fold_in(_tk, 803), (256, 1), jnp.float32)
        b_top1 = jnp.zeros((512,), jnp.float32)
        b_top2 = jnp.zeros((256,), jnp.float32)
        return (dense_ctx, ids, tbl_0, tbl_1, tbl_2, tbl_3, tbl_4, tbl_5, tbl_6, tbl_7, tbl_8, tbl_9, tbl_10, tbl_11, tbl_12, tbl_13, tbl_14, tbl_15, tbl_16, tbl_17, tbl_18, tbl_19, tbl_20, tbl_21, tbl_22, tbl_23, tbl_24, tbl_25, tbl_26, tbl_27, tbl_28, tbl_29, tbl_30, tbl_31, W_top1, b_top1, W_top2, b_top2, W_top3)
    dense_ctx, ids, tbl_0, tbl_1, tbl_2, tbl_3, tbl_4, tbl_5, tbl_6, tbl_7, tbl_8, tbl_9, tbl_10, tbl_11, tbl_12, tbl_13, tbl_14, tbl_15, tbl_16, tbl_17, tbl_18, tbl_19, tbl_20, tbl_21, tbl_22, tbl_23, tbl_24, tbl_25, tbl_26, tbl_27, tbl_28, tbl_29, tbl_30, tbl_31, W_top1, b_top1, W_top2, b_top2, W_top3 = _rec_inputs()

    def _L0_rec_setup():
        import jax, jax.numpy as jnp
        import numpy as np
        B, F, D = (512, 32, 32)
        LAYER_SIZE = [128, 128]

        def _cin_forward(inputs, filters):
            x0 = inputs
            prev = inputs
            outs = []
            for W in filters:
                z = jnp.einsum('bhd,bmd->bhmd', x0, prev)
                b, h, m, d = z.shape
                z = z.reshape(b, h * m, d)
                cur = jnp.einsum('bpd,pn->bnd', z, W[0])
                cur = jax.nn.relu(cur)
                prev = cur
                outs.append(cur)
            result = jnp.concatenate(outs, axis=1)
            return jnp.sum(result, axis=-1)
        key = jax.random.key(seed)
        k1, k2, k3 = jax.random.split(key, 3)
        inputs = jax.random.normal(k1, (B, F, D), dtype=jnp.float32)
        field_nums = [F] + LAYER_SIZE
        filter_0 = jax.random.normal(k2, (1, field_nums[0] * field_nums[0], field_nums[1]), dtype=jnp.float32) * 0.05
        filter_1 = jax.random.normal(k3, (1, field_nums[0] * field_nums[1], field_nums[2]), dtype=jnp.float32) * 0.05
        return {'inputs': inputs, 'filter_0': filter_0, 'filter_1': filter_1}
    _L0_rec_all = _L0_rec_setup()
    _L0_rec_in = {k: v for k, v in _L0_rec_all.items() if k in ('filter_0', 'filter_1')}
    del _L0_rec_all
    return {'dense_ctx': dense_ctx, 'ids': ids, 'tbl_0': tbl_0, 'tbl_1': tbl_1, 'tbl_2': tbl_2, 'tbl_3': tbl_3, 'tbl_4': tbl_4, 'tbl_5': tbl_5, 'tbl_6': tbl_6, 'tbl_7': tbl_7, 'tbl_8': tbl_8, 'tbl_9': tbl_9, 'tbl_10': tbl_10, 'tbl_11': tbl_11, 'tbl_12': tbl_12, 'tbl_13': tbl_13, 'tbl_14': tbl_14, 'tbl_15': tbl_15, 'tbl_16': tbl_16, 'tbl_17': tbl_17, 'tbl_18': tbl_18, 'tbl_19': tbl_19, 'tbl_20': tbl_20, 'tbl_21': tbl_21, 'tbl_22': tbl_22, 'tbl_23': tbl_23, 'tbl_24': tbl_24, 'tbl_25': tbl_25, 'tbl_26': tbl_26, 'tbl_27': tbl_27, 'tbl_28': tbl_28, 'tbl_29': tbl_29, 'tbl_30': tbl_30, 'tbl_31': tbl_31, 'W_top1': W_top1, 'b_top1': b_top1, 'W_top2': W_top2, 'b_top2': b_top2, 'W_top3': W_top3, 'L0_rec_filter_0': _L0_rec_in['filter_0'], 'L0_rec_filter_1': _L0_rec_in['filter_1']}

def reference(dense_ctx, ids, tbl_0, tbl_1, tbl_2, tbl_3, tbl_4, tbl_5, tbl_6, tbl_7, tbl_8, tbl_9, tbl_10, tbl_11, tbl_12, tbl_13, tbl_14, tbl_15, tbl_16, tbl_17, tbl_18, tbl_19, tbl_20, tbl_21, tbl_22, tbl_23, tbl_24, tbl_25, tbl_26, tbl_27, tbl_28, tbl_29, tbl_30, tbl_31, W_top1, b_top1, W_top2, b_top2, W_top3, L0_rec_filter_0, L0_rec_filter_1):
    import jax
    import jax.numpy as jnp

    def _L0_rec_ref(inputs, filter_0, filter_1):
        import jax, jax.numpy as jnp
        import numpy as np
        B, F, D = (512, 32, 32)
        LAYER_SIZE = [128, 128]

        def _cin_forward(inputs, filters):
            x0 = inputs
            prev = inputs
            outs = []
            for W in filters:
                z = jnp.einsum('bhd,bmd->bhmd', x0, prev)
                b, h, m, d = z.shape
                z = z.reshape(b, h * m, d)
                cur = jnp.einsum('bpd,pn->bnd', z, W[0])
                cur = jax.nn.relu(cur)
                prev = cur
                outs.append(cur)
            result = jnp.concatenate(outs, axis=1)
            return jnp.sum(result, axis=-1)
        return _cin_forward(inputs, (filter_0, filter_1))
    e = jnp.stack([tbl_0[ids[:, 0]], tbl_1[ids[:, 1]], tbl_2[ids[:, 2]], tbl_3[ids[:, 3]], tbl_4[ids[:, 4]], tbl_5[ids[:, 5]], tbl_6[ids[:, 6]], tbl_7[ids[:, 7]], tbl_8[ids[:, 8]], tbl_9[ids[:, 9]], tbl_10[ids[:, 10]], tbl_11[ids[:, 11]], tbl_12[ids[:, 12]], tbl_13[ids[:, 13]], tbl_14[ids[:, 14]], tbl_15[ids[:, 15]], tbl_16[ids[:, 16]], tbl_17[ids[:, 17]], tbl_18[ids[:, 18]], tbl_19[ids[:, 19]], tbl_20[ids[:, 20]], tbl_21[ids[:, 21]], tbl_22[ids[:, 22]], tbl_23[ids[:, 23]], tbl_24[ids[:, 24]], tbl_25[ids[:, 25]], tbl_26[ids[:, 26]], tbl_27[ids[:, 27]], tbl_28[ids[:, 28]], tbl_29[ids[:, 29]], tbl_30[ids[:, 30]], tbl_31[ids[:, 31]]], axis=1)
    z = _L0_rec_ref(e, L0_rec_filter_0, L0_rec_filter_1)
    z = z.reshape(z.shape[0], -1)
    h = jnp.concatenate([z, dense_ctx], axis=1)
    h = jnp.maximum(h @ W_top1 + b_top1, 0.0)
    h = jnp.maximum(h @ W_top2 + b_top2, 0.0)
    y = h @ W_top3
    return y

_drawn_inputs = setup_inputs


def setup_inputs(seed=0):
    import zlib

    import numpy as np

    out = dict(_drawn_inputs(seed))
    spreads = {'b_top1': (0.0, 0.434), 'b_top2': (0.0, 0.427)}
    factors = {'tbl_0': 6.035,
     'tbl_1': 5.982,
     'tbl_2': 6.174,
     'tbl_3': 6.432,
     'tbl_4': 6.187,
     'tbl_5': 6.234,
     'tbl_6': 6.238,
     'tbl_7': 6.036,
     'tbl_8': 6.042,
     'tbl_9': 5.811,
     'tbl_10': 5.89,
     'tbl_11': 6.028,
     'tbl_12': 5.803,
     'tbl_13': 5.606,
     'tbl_14': 5.826,
     'tbl_15': 5.834,
     'tbl_16': 6.425,
     'tbl_17': 6.16,
     'tbl_18': 5.868,
     'tbl_19': 6.179,
     'tbl_20': 6.073,
     'tbl_21': 5.839,
     'tbl_22': 6.203,
     'tbl_23': 6.153,
     'tbl_24': 6.484,
     'tbl_25': 6.02,
     'tbl_26': 5.805,
     'tbl_27': 6.062,
     'tbl_28': 6.336,
     'tbl_29': 6.013,
     'tbl_30': 6.137,
     'tbl_31': 5.783,
     'L0_rec_filter_1': 8.0}
    for name, (base, spread) in spreads.items():
        noise = np.random.default_rng([zlib.crc32(name.encode()), seed]).standard_normal(out[name].shape)
        drawn = base * np.exp(spread * noise) if base else spread * noise
        out[name] = jnp.asarray(drawn.astype(out[name].dtype))
    for name, factor in factors.items():
        out[name] = (out[name] * factor).astype(out[name].dtype)
    return out
```

```python
from contextlib import ExitStack

import concourse.bass as bass
from concourse import mybir

F32 = mybir.dt.float32
F32R = mybir.dt.float32r
BF16 = mybir.dt.bfloat16
I32 = mybir.dt.int32
U32 = mybir.dt.uint32
ALU = mybir.AluOpType
ACT = mybir.ActivationFunctionType
AX = mybir.AxisListType

P = 128
FIELDS = 32
DIM = 32
BATCH = 1024
N1 = 128
N2 = 128
COLS = 512
B_TILE = COLS // DIM
TILES = BATCH // B_TILE
BLOCKS = BATCH // P
T_BLOCK = TILES // BLOCKS
PARTS = 3
XROWS = PARTS * FIELDS
H_CHUNK = 4
M_CHUNK = P // H_CHUNK
GROUPS = FIELDS // H_CHUNK
MG = N1 // M_CHUNK
GCOLS = MG * COLS
SHIFTS = FIELDS // 2 // H_CHUNK
HALF = FIELDS // 2
AHEAD = 4

MODES = "PFPPVPFP"
FULL = [g for g in range(GROUPS) if MODES[g] == "F"]
SPLIT = [g for g in range(GROUPS) if MODES[g] != "F"]
ON_POOL = [g for g in range(GROUPS) if MODES[g] == "P"]
ON_DVE = [g for g in range(GROUPS) if MODES[g] == "V"]
Z_RING = 4
HI_RING = 4
LO_RING = 3
assert GROUPS % Z_RING == 0 and AHEAD == Z_RING
assert 2 * len(SPLIT) % HI_RING == 0 and 2 * len(SPLIT) % LO_RING == 0

TOP1 = 512
TOP2 = 256
CTX = 16


def split_before(g, k):
    r = SPLIT.index(g) - k
    return r // len(SPLIT), SPLIT[r % len(SPLIT)]


def build_dlrm(nc, ctx_t, ids, tables, w_top1, b_top1, w_top2, b_top2, w_top3, filt0, filt0_t, filt1, selectors, out):
    es = ExitStack()
    with es:
        def sb(name, shape, dt):
            return es.enter_context(nc.sbuf_tensor(name, shape, dt))

        def sem(name):
            return es.enter_context(nc.semaphore(name))

        ids_sb = sb("ids_sb", [P, BLOCKS, FIELDS], I32)
        idx_now = sb("idx_now", [P, FIELDS], I32)
        emb = sb("emb", [P, FIELDS, DIM], F32)
        emb_t = sb("emb_t", [P, DIM, 32], F32)
        parts = sb("parts", [P, PARTS, 2, DIM, B_TILE], BF16)
        xs = sb("xs", [XROWS, 2 * T_BLOCK * COLS], BF16)
        sel = sb("sel", [XROWS, 14, P], BF16)
        rep = sb("rep", [P, COLS], F32)
        z1 = sb("z1", [P, MG, COLS], F32)
        z1_half = sb("z1_half", [HALF, COLS], F32)
        w0 = sb("w0", [P, SHIFTS + 1, N1], F32)
        w0_t = sb("w0_t", [P, SHIFTS + 1, N1], F32)
        w1_hi = sb("w1_hi", [P, GROUPS, MG, N2], F32R)
        w1_lo = sb("w1_lo", [P, GROUPS, MG, N2], F32R)
        w1_full = sb("w1_full", [P, len(FULL), MG, N2], F32)
        prev = sb("prev", [P, 2, COLS], F32)
        prev_rep = sb("prev_rep", [P, 2, MG, COLS], F32)
        z = sb("z", [P, Z_RING, GCOLS], F32)
        z_hi = sb("z_hi", [P, HI_RING, GCOLS], F32R)
        z_lo = sb("z_lo", [P, LO_RING, GCOLS], F32R)
        cur2 = sb("cur2", [P, DIM, B_TILE], F32)
        sums = sb("sums", [P, 2, BATCH], F32)
        bias1 = sb("bias1", [P, TOP1 // P], F32)
        bias2 = sb("bias2", [P, TOP2 // P], F32)
        w3 = sb("w3", [P, TOP2 // P], F32)
        t1_w = z[:, 0, 0:2 * TOP1].rearrange("p (k n) -> p k n", k=2)
        t1_wc = z[0:CTX, 0, 2 * TOP1:3 * TOP1]
        t2_w = z[:, 1, 0:4 * TOP2].rearrange("p (k n) -> p k n", k=4)
        ctx_sb = z[0:CTX, 1, 4 * TOP2:4 * TOP2 + BATCH]
        y = emb_t[0:1, :, :].rearrange("p d b -> p (d b)")
        ps = es.enter_context(nc.psum_tensor("ps", [P, 8, COLS], F32))
        X_BANK, S_BANK, ACC1, ACC2 = 0, 2, 4, 6

        ids_in = sem("ids_in")
        w0_in = sem("w0_in")
        w1_in = sem("w1_in")
        sel_in = sem("sel_in")
        small_in = sem("small_in")
        tower_in = sem("tower_in")
        idx_ready = sem("idx_ready")
        gathered = sem("gathered")
        emb_taken = sem("emb_taken")
        prep_step = sem("prep_step")
        parts_ready = sem("parts_ready")
        xs_ready = sem("xs_ready")
        sel_ready = sem("sel_ready")
        w0_ready = sem("w0_ready")
        w1_hi_ready = sem("w1_hi_ready")
        w1_lo_ready = sem("w1_lo_ready")
        s_ready = sem("s_ready")
        rep_ready = sem("rep_ready")
        z1_ready = sem("z1_ready")
        l1_done = sem("l1_done")
        relu1_done = sem("relu1_done")
        sum1_done = sem("sum1_done")
        rep_in = [sem(f"rep_in_{x}") for x in ("even", "odd")]
        x_ready = sem("x_ready")
        z_ready = sem("z_ready")
        hi_ready = sem("hi_ready")
        lo_pool = sem("lo_pool")
        lo_dve = sem("lo_dve")
        mm_done = sem("mm_done")
        acc2_free = sem("acc2_free")
        cur2_free = sem("cur2_free")
        t_mm = sem("t_mm")
        t_act = sem("t_act")
        y_out = sem("y_out")

        REP_DMAS = H_CHUNK * MG
        XS_DMAS = 4 * PARTS

        def groups_to(t, g):
            return GROUPS * t + (g + 1)

        def norm(t, g):
            return (t, g) if g < GROUPS else (t + 1, g - GROUPS)

        def rank(kind, t, g):
            return len(kind) * t + (kind.index(g) + 1)

        def ring(parity, g, size):
            return (len(SPLIT) * parity + SPLIT.index(g)) % size

        def every_tile(eng, tile):
            tile(0, 0, True)
            with eng.Fori(0, (TILES - 4) // 2) as i:
                tile(2 * i + 1, 1, True)
                tile(2 * i + 2, 0, True)
            tile(TILES - 3, 1, True)
            tile(TILES - 2, 0, False)
            tile(TILES - 1, 1, False)

        def every_tile_by_block(eng, tile, between):
            tile(0, 0, True)
            with eng.Fori(0, BLOCKS - 1) as k:
                with eng.Fori(0, 2) as i:
                    tile(T_BLOCK * k + 2 * i + 1, 1, True)
                    tile(T_BLOCK * k + 2 * i + 2, 0, True)
                between(k + 1)
                with eng.Fori(0, 2) as i:
                    tile(T_BLOCK * k + 2 * i + 5, 1, True)
                    tile(T_BLOCK * k + 2 * i + 6, 0, True)
            with eng.Fori(0, 2) as i:
                tile(TILES - T_BLOCK + 2 * i + 1, 1, True)
                tile(TILES - T_BLOCK + 2 * i + 2, 0, True)
            tile(TILES - 3, 1, True)
            tile(TILES - 2, 0, False)
            tile(TILES - 1, 1, False)

        block = es.enter_context(nc.Block())

        @block.sync
        def _(sp):
            sp.dma_start(ids_sb[:], ids.rearrange("(k p) f -> p k f", p=P)).then_inc(ids_in, 16)
            sp.dma_start(z[0:XROWS, 2, 0:14 * P], selectors).then_inc(sel_in, 16)
            sp.dma_start(w0[:], filt0).then_inc(w0_in, 16)
            sp.dma_start(w0_t[:], filt0_t).then_inc(w0_in, 16)
            sp.dma_start(z[:, 0:2, :], filt1.rearrange("p (r c) -> p r c", r=2)).then_inc(w1_in, 16)
            for n, g in enumerate(FULL):
                sp.dma_start(w1_full[:, n, :, :].rearrange("p m n -> p (m n)"),
                             filt1[:, g * MG * N2:(g + 1) * MG * N2]).then_inc(small_in, 16)
            with nc.allow_non_contiguous_dma(reason="a few hundred bias and weight elements"):
                sp.dma_start(bias1[:], b_top1.rearrange("(c p) -> p c", p=P)).then_inc(small_in, 16)
                sp.dma_start(bias2[:], b_top2.rearrange("(c p) -> p c", p=P)).then_inc(small_in, 16)
                sp.dma_start(w3[:], w_top3.rearrange("(c p) o -> p (c o)", p=P)).then_inc(small_in, 16)

            def value(x):
                return x if isinstance(x, int) else sp.snap(x)

            def spread_parts(k):
                ready = value(k + 1)
                places = [value((k % 2) * (T_BLOCK * COLS) + q * 2 * COLS) for q in range(4)]
                sp.wait_ge(parts_ready, ready)
                for q, at in enumerate(places):
                    for part in range(PARTS):
                        sp.dma_start(xs[part * FIELDS:(part + 1) * FIELDS, bass.ds(at, 2 * COLS)],
                                     parts[q * 32:(q + 1) * 32, part, :, :, :].rearrange("p s d b -> p (s d b)")
                                     ).then_inc(xs_ready, 16)

            def repeat_prev(t, parity, first=False):
                ready, used = value(t + 1), value(GROUPS * (t - 1))
                sp.wait_ge(relu1_done, ready)
                if not first:
                    sp.wait_ge(z_ready, used)
                for m in range(MG):
                    for r in range(H_CHUNK):
                        sp.dma_start(prev_rep[r * M_CHUNK:(r + 1) * M_CHUNK, parity, m, :],
                                     prev[m * M_CHUNK:(m + 1) * M_CHUNK, parity, :]).then_inc(rep_in[parity], 16)

            spread_parts(0)
            repeat_prev(0, 0, True)
            repeat_prev(1, 1, True)

            def tile(t, parity, more):
                if more:
                    repeat_prev(t + 2, parity)

            every_tile_by_block(sp, tile, spread_parts)
            sp.wait_ge(mm_done, GROUPS * (TILES - 1) + 6)
            sp.dma_start(t1_w, w_top1[0:2 * P, :].rearrange("(k p) n -> p k n", p=P)).then_inc(tower_in, 16)
            sp.dma_start(t1_wc, w_top1[2 * P:2 * P + CTX, :]).then_inc(tower_in, 16)
            sp.dma_start(ctx_sb, ctx_t).then_inc(tower_in, 16)
            sp.dma_start(t2_w, w_top2.rearrange("(k p) n -> p k n", p=P)).then_inc(tower_in, 16)
            sp.wait_ge(t_act, 14)
            sp.dma_start(out.rearrange("b o -> o b"), y).then_inc(y_out, 16)
            sp.wait_ge(y_out, 16)

        @block.gpsimd
        def _(pool):
            def gather(k, fields, idx):
                for f in fields:
                    nc.gpsimd.indirect_dma_start(
                        emb[:, f, :], None, tables[f],
                        bass.IndirectOffsetOnAxis(idx[:, f:f + 1].bitcast(U32), 0)).then_inc(gathered, 16)

            pool.wait_ge(ids_in, 16)
            gather(0, range(FIELDS), ids_sb[:, 0, :])
            nc.gpsimd.tensor_copy(idx_now[:], ids_sb[:, 1, :]).then_inc(idx_ready, 1)
            pool.wait_ge(idx_ready, 1)
            pool.wait_ge(emb_taken, 1)
            gather(1, range(FIELDS // 2), idx_now)

            def low_part(t, g, parity, first=False):
                if g not in ON_POOL:
                    return
                pool.wait_ge(hi_ready, rank(SPLIT, t, g))
                back, used = split_before(g, LO_RING)
                if not first:
                    pool.wait_ge(mm_done, groups_to(t + back, used))
                nc.gpsimd.tensor_tensor(z_lo[:, ring(parity, g, LO_RING), :], z[:, g % Z_RING, :],
                                        z_hi[:, ring(parity, g, HI_RING), :].bitcast(F32),
                                        ALU.subtract).then_inc(lo_pool, 1)

            for g in range(AHEAD):
                low_part(0, g, 0, SPLIT.index(g) < LO_RING if g in SPLIT else True)

            def tile(t, parity, last=False, gathers=None):
                for g in range(GROUPS):
                    if not last or g + AHEAD < GROUPS:
                        tt, gg = norm(t, g + AHEAD)
                        low_part(tt, gg, parity if g + AHEAD < GROUPS else 1 - parity)
                    if gathers is not None and g % 2 == 1:
                        gathers((g - 1) // 2)

            def pace(k, n):
                def some(j):
                    gather(k, [4 * n + j], idx_now)
                return some

            def half_before(k):
                for n in range(4):
                    tile(T_BLOCK * k + n + 1, (n + 1) % 2, gathers=pace(k + 1, 4 + n))

            def half_after(k, more):
                if more:
                    pool.wait_ge(gathered, 16 * FIELDS * (k + 2))
                    nc.gpsimd.tensor_copy(idx_now[:], ids_sb[:, bass.ds(k + 2, 1), :].rearrange(
                        "p o f -> p (o f)")).then_inc(idx_ready, 1)
                    pool.wait_ge(idx_ready, k + 2)
                    pool.wait_ge(emb_taken, k + 2)
                for n in range(4):
                    tile(T_BLOCK * k + n + 5, (n + 1) % 2, gathers=pace(k + 2, n) if more else None)

            tile(0, 0)
            with pool.Fori(0, BLOCKS - 2) as k:
                half_before(k)
                half_after(k, True)
            half_before(BLOCKS - 2)
            half_after(BLOCKS - 2, False)
            with pool.Fori(0, (T_BLOCK - 2) // 2) as i:
                tile(TILES - T_BLOCK + 2 * i + 1, 1)
                tile(TILES - T_BLOCK + 2 * i + 2, 0)
            tile(TILES - 1, 1, last=True)

        @block.scalar
        def _(act):
            act.wait_ge(sel_in, 16)
            nc.scalar.activation(sel[:].rearrange("p k n -> p (k n)"), z[0:XROWS, 2, 0:14 * P],
                                 ACT.Copy).then_inc(sel_ready, 1)
            act.wait_ge(w1_in, 16)
            nc.scalar.activation(w1_hi[:].rearrange("p (r g) m n -> p r (g m n)", r=2), z[:, 0:2, :],
                                 ACT.Copy).then_inc(w1_hi_ready, 1)
            act.wait_ge(w1_hi_ready, 1)
            act.sem_inc(acc2_free, 2)

            def take_rep(t, first=False):
                act.wait_ge(s_ready, 4 * t + 1)
                if not first:
                    act.wait_ge(z1_ready, 3 * t)
                nc.scalar.activation(rep[:], ps[:, S_BANK, :], ACT.Copy).then_inc(rep_ready, 1)

            def relu1(t, parity, first=False):
                act.wait_ge(l1_done, t + 1)
                if not first:
                    act.wait_ge(rep_in[parity], 16 * REP_DMAS * (t // 2))
                    act.wait_ge(sum1_done, t - 1)
                nc.scalar.activation(prev[:, parity, :], ps[:, ACC1 + parity, :], ACT.Relu).then_inc(relu1_done, 1)

            def relu2(t, parity):
                act.wait_ge(mm_done, GROUPS * (t + 1))
                act.wait_ge(cur2_free, t + 1)
                nc.scalar.activation(cur2[:].rearrange("p d b -> p (d b)"), ps[:, ACC2 + parity, :],
                                     ACT.Relu).then_inc(acc2_free, 1)

            def high_part(t, g, parity, first=False):
                if g not in SPLIT:
                    return
                act.wait_ge(z_ready, groups_to(t, g))
                back, used = split_before(g, HI_RING)
                if not first:
                    act.wait_ge(mm_done, groups_to(t + back, used))
                nc.scalar.activation(z_hi[:, ring(parity, g, HI_RING), :], z[:, g % Z_RING, :],
                                     ACT.Copy).then_inc(hi_ready, 1)

            take_rep(0, True)
            relu1(0, 0, True)
            take_rep(1)
            relu1(1, 1, True)
            for g in range(AHEAD):
                high_part(0, g, 0, True)

            def tile(t, parity, more):
                for g in range(GROUPS):
                    if more and g == 0:
                        take_rep(t + 2)
                    if g == 1 and not (isinstance(t, int) and t == 0):
                        relu2(t - 1, 1 - parity)
                    if not (isinstance(t, int) and t == TILES - 1) or g + AHEAD < GROUPS:
                        tt, gg = norm(t, g + AHEAD)
                        first = isinstance(t, int) and t == 0 and g + AHEAD < GROUPS and SPLIT.index(gg) < HI_RING if gg in SPLIT else False
                        high_part(tt, gg, parity if g + AHEAD < GROUPS else 1 - parity, first)
                    if more and g == 6:
                        relu1(t + 2, parity)

            every_tile(act, tile)
            relu2(TILES - 1, 1)

            act.wait_ge(small_in, 16 * (3 + len(FULL)))
            act.wait_ge(mm_done, GROUPS * TILES)
            for half in range(2):
                for o in range(4):
                    act.wait_ge(t_mm, 4 * half + o + 1)
                    nc.scalar.activation(z[:, 2 + half, o * COLS:(o + 1) * COLS], ps[:, 4 * half + o, :],
                                         ACT.Relu, bias=bias1[:, o:o + 1]).then_inc(t_act, 1)
            for half in range(2):
                for o in range(2):
                    act.wait_ge(t_mm, 8 + 2 * half + o + 1)
                    nc.scalar.activation(z1[:, 2 * half + o, :], ps[:, 2 * half + o, :],
                                         ACT.Relu, bias=bias2[:, o:o + 1]).then_inc(t_act, 1)
            for half in range(2):
                act.wait_ge(t_mm, 12 + half + 1)
                nc.scalar.activation(y[0:1, half * COLS:(half + 1) * COLS], ps[0:1, 4 + half, :],
                                     ACT.Copy).then_inc(t_act, 1)

        @block.vector
        def _(dve):
            steps = [0]

            def prepare(k):
                dve.wait_ge(gathered, 16 * FIELDS * (k + 1))
                nc.vector.transpose(emb_t[:], emb[:].rearrange("p h d -> p d h")).then_inc(emb_taken, 1)
                dve.wait_ge(emb_taken, k + 1)
                if not isinstance(k, int) or k:
                    dve.wait_ge(xs_ready, 16 * XS_DMAS * k)
                view = emb_t[:].rearrange("p d (s b) -> p s d b", s=2)
                for part in range(PARTS):
                    nc.vector.tensor_copy(parts[:, part, :, :, :], view).then_inc(
                        parts_ready if part == PARTS - 1 else prep_step, 1)
                    if part < PARTS - 1:
                        dve.wait_ge(prep_step, 4 * k + 2 * part + 1)
                        for s in range(2):
                            last = nc.vector.tensor_tensor(view[:, s, :, :], view[:, s, :, :],
                                                           parts[:, part, s, :, :], ALU.subtract)
                        last.then_inc(prep_step, 1)
                        dve.wait_ge(prep_step, 4 * k + 2 * part + 2)

            def z1_part(t, n, first=False):
                dve.wait_ge(s_ready, 4 * t + 2 + n)
                if n == 0:
                    dve.wait_ge(rep_ready, t + 1)
                    if not first:
                        dve.wait_ge(l1_done, t)
                if n < 2:
                    nc.vector.tensor_tensor(z1[:, 2 * n:2 * n + 2, :], ps[:, S_BANK:S_BANK + 2, :],
                                            rep[:, None, :].to_broadcast([P, 2, COLS]), ALU.mult).then_inc(z1_ready, 1)
                else:
                    nc.vector.tensor_tensor(z1_half[:], ps[0:HALF, S_BANK, :], rep[0:HALF, :],
                                            ALU.mult).then_inc(z1_ready, 1)

            def sum1(t, parity):
                dve.wait_ge(relu1_done, t + 1)
                nc.vector.tensor_reduce(sums[:, 0, bass.ds(B_TILE * t, B_TILE)],
                                        prev[:, parity, :].rearrange("p (d b) -> p b d", d=DIM),
                                        AX.X, ALU.add).then_inc(sum1_done, 1)

            def sum2(t):
                dve.wait_ge(acc2_free, t + 3)
                nc.vector.tensor_reduce(sums[:, 1, bass.ds(B_TILE * t, B_TILE)],
                                        cur2[:].rearrange("p d b -> p b d"), AX.X, ALU.add).then_inc(cur2_free, 1)

            def product(t, g, parity, first=False):
                dve.wait_ge(x_ready, groups_to(t, g))
                if g == 0:
                    dve.wait_ge(rep_in[parity], 16 * REP_DMAS * (t // 2 + 1))
                if not first:
                    tb, gb = (t, g - Z_RING) if g >= Z_RING else (t - 1, g + GROUPS - Z_RING)
                    if gb in FULL:
                        dve.wait_ge(mm_done, groups_to(tb, gb))
                    elif gb in ON_POOL:
                        dve.wait_ge(lo_pool, rank(ON_POOL, tb, gb))
                    else:
                        dve.wait_ge(lo_dve, rank(ON_DVE, tb, gb))
                nc.vector.tensor_tensor(z[:, g % Z_RING, :].rearrange("p (m c) -> p m c", m=MG),
                                        ps[:, X_BANK + g % 2, None, :].to_broadcast([P, MG, COLS]),
                                        prev_rep[:, parity, :, :], ALU.mult).then_inc(z_ready, 1)

            def low_part(t, g, parity, first=False):
                if g not in ON_DVE:
                    return
                dve.wait_ge(hi_ready, rank(SPLIT, t, g))
                back, used = split_before(g, LO_RING)
                if not first:
                    dve.wait_ge(mm_done, groups_to(t + back, used))
                nc.vector.tensor_tensor(z_lo[:, ring(parity, g, LO_RING), :], z[:, g % Z_RING, :],
                                        z_hi[:, ring(parity, g, HI_RING), :].bitcast(F32),
                                        ALU.subtract).then_inc(lo_dve, 1)

            nc.vector.memset(cur2[:], 0.0).then_inc(cur2_free, 1)
            dve.wait_ge(w0_in, 32)
            nc.vector.tensor_tensor(w0[:], w0[:], w0_t[:], ALU.add).then_inc(w0_ready, 1)
            dve.wait_ge(w1_hi_ready, 1)
            nc.vector.tensor_tensor(w1_lo[:].rearrange("p (r g) m n -> p r (g m n)", r=2), z[:, 0:2, :],
                                    w1_hi[:].rearrange("p (r g) m n -> p r (g m n)", r=2).bitcast(F32),
                                    ALU.subtract).then_inc(w1_lo_ready, 1)
            dve.wait_ge(w1_lo_ready, 1)
            dve.wait_ge(sel_ready, 1)
            prepare(0)
            for t in range(2):
                for n in range(3):
                    z1_part(t, n, t == 0)
                sum1(t, t)
            for g in range(AHEAD):
                product(0, g, 0, True)
                if g:
                    low_part(0, g - 1, 0, True)

            def tile(t, parity, more):
                last = isinstance(t, int) and t == TILES - 1
                for g in range(GROUPS):
                    if more and 1 <= g <= 3:
                        z1_part(t + 2, g - 1)
                    if g == 4 and not (isinstance(t, int) and t == 0):
                        sum2(t - 1)
                    if not last or g + AHEAD < GROUPS:
                        tt, gg = norm(t, g + AHEAD)
                        product(tt, gg, parity if g + AHEAD < GROUPS else 1 - parity)
                    if not last or g + AHEAD - 1 < GROUPS:
                        tt, gg = norm(t, g + AHEAD - 1)
                        first = isinstance(t, int) and t == 0 and g + AHEAD - 1 < GROUPS and gg in SPLIT and SPLIT.index(gg) < LO_RING
                        low_part(tt, gg, parity if g + AHEAD - 1 < GROUPS else 1 - parity, first)
                    if more and g == 7:
                        sum1(t + 2, parity)

            every_tile_by_block(dve, tile, prepare)
            sum2(TILES - 1)

        @block.tensor
        def _(pe):
            def columns(t):
                return xs[:, bass.ds((t % (2 * T_BLOCK)) * COLS, COLS)]

            def spread(bank, form, t):
                return nc.tensor.matmul(ps[:, bank, :], sel[:, form, :], columns(t), start=True, stop=True)

            def l1_piece(t, n, first=False):
                if n == 0:
                    pe.wait_ge(xs_ready, 16 * XS_DMAS * (t // T_BLOCK + 1))
                    if not first:
                        pe.wait_ge(z1_ready, 3 * t)
                    spread(S_BANK, GROUPS, t).then_inc(s_ready, 1)
                elif n == 1:
                    pe.wait_ge(rep_ready, t + 1)
                    spread(S_BANK, GROUPS + 1, t)
                    spread(S_BANK + 1, GROUPS + 2, t).then_inc(s_ready, 1)
                elif n == 2:
                    pe.wait_ge(z1_ready, 3 * t + 1)
                    spread(S_BANK, GROUPS + 3, t)
                    spread(S_BANK + 1, GROUPS + 4, t).then_inc(s_ready, 1)
                else:
                    pe.wait_ge(z1_ready, 3 * t + 2)
                    spread(S_BANK, GROUPS + 5, t).then_inc(s_ready, 1)

            def l1_matmuls(t, parity, first=False):
                pe.wait_ge(z1_ready, 3 * t + 3)
                if not first:
                    pe.wait_ge(relu1_done, t - 1)
                for s in range(SHIFTS):
                    nc.tensor.matmul(ps[:, ACC1 + parity, :], w0[:, s, :], z1[:, s, :], start=(s == 0), stop=False)
                nc.tensor.matmul(ps[:, ACC1 + parity, :], w0[0:HALF, SHIFTS, :], z1_half[:],
                                 start=False, stop=True).then_inc(l1_done, 1)

            def x_form(t, g, first=False):
                if not first:
                    pe.wait_ge(z_ready, groups_to(t, g - 2))
                spread(X_BANK + g % 2, g, t).then_inc(x_ready, 1)

            def group(t, g, parity):
                acc = ps[:, ACC2 + parity, :]
                if g in FULL:
                    pe.wait_ge(z_ready, groups_to(t, g))
                    for m in range(MG):
                        last = nc.tensor.matmul(acc, w1_full[:, FULL.index(g), m, :],
                                                z[:, g % Z_RING, m * COLS:(m + 1) * COLS],
                                                start=(g == 0 and m == 0), stop=(g == GROUPS - 1 and m == MG - 1))
                else:
                    hi = z_hi[:, ring(parity, g, HI_RING), :]
                    lo = z_lo[:, ring(parity, g, LO_RING), :]
                    pe.wait_ge(hi_ready, rank(SPLIT, t, g))
                    for m in range(MG):
                        c = slice(m * COLS, (m + 1) * COLS)
                        nc.tensor.matmul(acc, w1_lo[:, g, m, :], hi[:, c], start=(g == 0 and m == 0), stop=False)
                        nc.tensor.matmul(acc, w1_hi[:, g, m, :], hi[:, c], start=False, stop=False)
                    if g in ON_POOL:
                        pe.wait_ge(lo_pool, rank(ON_POOL, t, g))
                    else:
                        pe.wait_ge(lo_dve, rank(ON_DVE, t, g))
                    for m in range(MG):
                        c = slice(m * COLS, (m + 1) * COLS)
                        last = nc.tensor.matmul(acc, w1_hi[:, g, m, :], lo[:, c], start=False,
                                                stop=(g == GROUPS - 1 and m == MG - 1))
                last.then_inc(mm_done, 1)

            pe.wait_ge(sel_ready, 1)
            pe.wait_ge(w0_ready, 1)
            for t in range(2):
                for n in range(4):
                    l1_piece(t, n, t == 0)
                l1_matmuls(t, t, True)
            for g in range(AHEAD):
                x_form(0, g, g < 2)
            pe.wait_ge(w1_lo_ready, 1)
            pe.wait_ge(small_in, 16 * (3 + len(FULL)))

            def tile(t, parity, more):
                pe.wait_ge(acc2_free, t + 1)
                for g in range(GROUPS):
                    if more and g < 4:
                        l1_piece(t + 2, g)
                    if not (isinstance(t, int) and t == TILES - 1) or g + AHEAD < GROUPS:
                        x_form(*norm(t, g + AHEAD))
                    group(t, g, parity)
                    if more and g == 5:
                        l1_matmuls(t + 2, parity)

            every_tile(pe, tile)

            pe.wait_ge(tower_in, 64)
            pe.wait_ge(z_ready, GROUPS * TILES)
            for half in range(2):
                c = slice(half * COLS, (half + 1) * COLS)
                pe.wait_ge(cur2_free, TILES - 31 if half == 0 else TILES + 1)
                for o in range(4):
                    n = slice(o * P, (o + 1) * P)
                    acc = ps[:, 4 * half + o, :]
                    nc.tensor.matmul(acc, t1_wc[:, n], ctx_sb[:, c], start=True, stop=False)
                    nc.tensor.matmul(acc, t1_w[:, 0, n], sums[:, 0, c], start=False, stop=False)
                    nc.tensor.matmul(acc, t1_w[:, 1, n], sums[:, 1, c], start=False, stop=True).then_inc(t_mm, 1)
            for half in range(2):
                pe.wait_ge(t_act, 4 * (half + 1))
                for o in range(2):
                    for k in range(4):
                        last = nc.tensor.matmul(ps[:, 2 * half + o, :], t2_w[:, k, o * P:(o + 1) * P],
                                                z[:, 2 + half, k * COLS:(k + 1) * COLS], start=(k == 0), stop=(k == 3))
                    last.then_inc(t_mm, 1)
            for half in range(2):
                pe.wait_ge(t_act, 8 + 2 * (half + 1))
                for k in range(2):
                    last = nc.tensor.matmul(ps[0:1, 4 + half, :], w3[:, k:k + 1], z1[:, 2 * half + k, :],
                                            start=(k == 0), stop=(k == 1))
                last.then_inc(t_mm, 1)


def selector_matrix():
    import numpy as np
    sel = np.zeros((PARTS, FIELDS, 14, P), np.float32)
    for row in range(P):
        j, low = row // 32, row % 32
        for g in range(GROUPS):
            sel[:, H_CHUNK * g + j, g, row] = 1.0
        sel[:, low, GROUPS, row] = 1.0
        for s in range(SHIFTS + 1):
            sel[:, (low + H_CHUNK * s + j) % FIELDS, GROUPS + 1 + s, row] = 1.0
    return sel.reshape(XROWS, 14 * P)


def kernel(**inputs):
    import numpy as np
    import concourse.bacc as bacc
    from concourse.bass_utils import run_bass_kernel_spmd

    a = {name: np.ascontiguousarray(x) for name, x in inputs.items()}
    tables = [a[f"tbl_{f}"] for f in range(FIELDS)]
    w = a["L0_rec_filter_0"].reshape(FIELDS, FIELDS, N1)
    filt0 = np.zeros((P, SHIFTS + 1, N1), np.float32)
    filt0_t = np.zeros((P, SHIFTS + 1, N1), np.float32)
    for s in range(HALF + 1):
        for h in range(FIELDS if s < HALF else HALF):
            row, chunk = (s % H_CHUNK) * FIELDS + h, s // H_CHUNK
            filt0[row, chunk] = w[h, (h + s) % FIELDS]
            if s:
                filt0_t[row, chunk] = w[(h + s) % FIELDS, h]
    v = a["L0_rec_filter_1"].reshape(GROUPS, H_CHUNK, MG, M_CHUNK, N2)
    filt1 = np.ascontiguousarray(v.transpose(1, 3, 0, 2, 4)).reshape(P, GROUPS * MG * N2)
    arrays = {
        "ctx_t": np.ascontiguousarray(a["dense_ctx"].T), "ids_in_dram": a["ids"],
        "w_top1": a["W_top1"], "b_top1": a["b_top1"], "w_top2": a["W_top2"], "b_top2": a["b_top2"],
        "w_top3": a["W_top3"], "filt0": filt0, "filt0_t": filt0_t, "filt1": filt1,
        "selectors": selector_matrix(),
    }
    for f in range(FIELDS):
        arrays[f"table_{f}"] = tables[f]
    nc = bacc.Bacc("TRN2", target_bir_lowering=False, num_devices=1)
    d = {n: nc.dram_tensor(n, x.shape, mybir.dt.from_np(x.dtype), kind="ExternalInput").ap() for n, x in arrays.items()}
    out = nc.dram_tensor("y_dram", (BATCH, 1), F32, kind="ExternalOutput").ap()
    build_dlrm(nc, d["ctx_t"], d["ids_in_dram"], [d[f"table_{f}"] for f in range(FIELDS)], d["w_top1"], d["b_top1"],
               d["w_top2"], d["b_top2"], d["w_top3"], d["filt0"], d["filt0_t"], d["filt1"], d["selectors"], out)
    r = run_bass_kernel_spmd(nc, [arrays], core_ids=[0])
    return r.results[0]["y_dram"]
```

```python
from contextlib import ExitStack

import concourse.bass as bass
from concourse import mybir

F32 = mybir.dt.float32
F32R = mybir.dt.float32r
BF16 = mybir.dt.bfloat16
I32 = mybir.dt.int32
U32 = mybir.dt.uint32
ALU = mybir.AluOpType
ACT = mybir.ActivationFunctionType
AX = mybir.AxisListType

P = 128
FIELDS = 32
DIM = 32
BATCH = 1024
N1 = 128
N2 = 128
COLS = 512
B_TILE = COLS // DIM
TILES = BATCH // B_TILE
BLOCKS = BATCH // P
T_BLOCK = TILES // BLOCKS
PARTS = 3
XROWS = PARTS * FIELDS
H_CHUNK = 4
M_CHUNK = P // H_CHUNK
GROUPS = FIELDS // H_CHUNK
MG = N1 // M_CHUNK
GCOLS = MG * COLS
SHIFTS = FIELDS // 2 // H_CHUNK
HALF = FIELDS // 2

KINDS = "PVPFPPFP"
LEAD = {"P": 5, "V": 5, "F": 2}
FULL = [g for g in range(GROUPS) if KINDS[g] == "F"]
SPLIT = [g for g in range(GROUPS) if KINDS[g] != "F"]
ON_POOL = [g for g in range(GROUPS) if KINDS[g] == "P"]
ON_DVE = [g for g in range(GROUPS) if KINDS[g] == "V"]
Z_RING = 3
HI_RING = 4
LO_RING = 3
assert all(2 * len(SPLIT) % n == 0 for n in (Z_RING, HI_RING, LO_RING))
MAKES = [[((s + LEAD[kind]) // GROUPS, g) for kind in "FVP" for g in range(GROUPS)
          if KINDS[g] == kind and (s + LEAD[kind]) % GROUPS == g] for s in range(GROUPS)]
ORDER = [made for step in MAKES for made in step]
AHEAD_OF = {g: ahead for ahead, g in ORDER}
FIRST = [g for ahead, g in ORDER if ahead]
LAST = [g for ahead, g in ORDER if not ahead]
assert [g for _, g in ORDER if g in SPLIT] == sorted(SPLIT, key=lambda g: (AHEAD_OF[g], g))

TOP1 = 512
TOP2 = 256
CTX = 16


def split_before(g, k):
    r = SPLIT.index(g) - k
    return r // len(SPLIT), SPLIT[r % len(SPLIT)]


def build_dlrm(nc, ctx_t, ids, tables, w_top1, b_top1, w_top2, b_top2, w_top3, filt0, filt0_t, filt1, selectors, out):
    es = ExitStack()
    with es:
        def sb(name, shape, dt):
            return es.enter_context(nc.sbuf_tensor(name, shape, dt))

        def sem(name):
            return es.enter_context(nc.semaphore(name))

        ids_sb = sb("ids_sb", [P, BLOCKS, FIELDS], I32)
        idx_now = sb("idx_now", [P, FIELDS], I32)
        emb = sb("emb", [P, FIELDS, DIM], F32)
        emb_t = sb("emb_t", [P, DIM, 32], F32)
        parts = sb("parts", [P, PARTS, 2, DIM, B_TILE], BF16)
        xs = sb("xs", [XROWS, 2 * T_BLOCK * COLS], BF16)
        sel = sb("sel", [XROWS, 14, P], BF16)
        rep = sb("rep", [P, COLS], F32)
        z1 = sb("z1", [P, MG, COLS], F32)
        z1_half = sb("z1_half", [3 * 32, COLS], F32)
        half_hl = sb("half_hl", [3 * 32, COLS], F32R)
        w0_lhh = sb("w0_lhh", [3 * 32, N1], F32R)
        w0 = sb("w0", [P, SHIFTS + 1, N1], F32)
        w1_hi = sb("w1_hi", [P, GROUPS, MG, N2], F32R)
        w1_lo = sb("w1_lo", [P, GROUPS, MG, N2], F32R)
        w1_full = sb("w1_full", [P, len(FULL), MG, N2], F32)
        prev = sb("prev", [P, 2, MG, COLS], F32)
        z = sb("z", [P, Z_RING + 1, GCOLS], F32)
        z_hi = sb("z_hi", [P, HI_RING, GCOLS], F32R)
        z_lo = sb("z_lo", [P, LO_RING, GCOLS], F32R)
        cur2 = sb("cur2", [P, DIM, B_TILE], F32)
        sums = sb("sums", [P, 2, BATCH], F32)
        bias1 = sb("bias1", [P, TOP1 // P], F32)
        bias2 = sb("bias2", [P, TOP2 // P], F32)
        w3 = sb("w3", [P, TOP2 // P], F32)
        w0_t = z[:, Z_RING, 0:(SHIFTS + 1) * N1].rearrange("p (s n) -> p s n", n=N1)
        t1_w = z[:, 0, 0:2 * TOP1].rearrange("p (k n) -> p k n", k=2)
        t1_wc = z[0:CTX, 0, 2 * TOP1:3 * TOP1]
        t2_w = z[:, 1, 0:4 * TOP2].rearrange("p (k n) -> p k n", k=4)
        ctx_sb = z[0:CTX, 1, 4 * TOP2:4 * TOP2 + BATCH]
        y = emb_t[0:1, :, :].rearrange("p d b -> p (d b)")
        ps = es.enter_context(nc.psum_tensor("ps", [P, 8, COLS], F32))
        X_BANK, S_BANK, ACC1, ACC2 = 0, 2, 4, 6

        ids_in = sem("ids_in")
        w0_in = sem("w0_in")
        w1_in = sem("w1_in")
        sel_in = sem("sel_in")
        small_in = sem("small_in")
        tower_in = sem("tower_in")
        idx_ready = sem("idx_ready")
        gathered = sem("gathered")
        emb_taken = sem("emb_taken")
        prep_step = sem("prep_step")
        parts_ready = sem("parts_ready")
        xs_ready = sem("xs_ready")
        sel_ready = sem("sel_ready")
        w0_ready = sem("w0_ready")
        w1_hi_ready = sem("w1_hi_ready")
        w1_lo_ready = sem("w1_lo_ready")
        s_ready = sem("s_ready")
        rep_ready = sem("rep_ready")
        z1_ready = sem("z1_ready")
        half_hi = sem("half_hi")
        half_lo = sem("half_lo")
        w0_hi = sem("w0_hi")
        w0_lo = sem("w0_lo")
        l1_done = sem("l1_done")
        relu1_done = sem("relu1_done")
        sum1_done = sem("sum1_done")
        turned = [sem(f"turned_{x}") for x in ("even", "odd")]
        x_ready = sem("x_ready")
        z_ready = sem("z_ready")
        hi_ready = sem("hi_ready")
        lo_pool = sem("lo_pool")
        lo_dve = sem("lo_dve")
        mm_done = sem("mm_done")
        acc2_free = sem("acc2_free")
        cur2_free = sem("cur2_free")
        t_mm = sem("t_mm")
        t_act = sem("t_act")
        y_out = sem("y_out")

        TURN_DMAS = 2 * (MG - 1)
        XS_DMAS = 4 * PARTS

        def groups_to(t, g):
            return GROUPS * t + (g + 1)

        def made_to(t, g):
            if isinstance(t, int) and t == 0 and AHEAD_OF[g]:
                return FIRST.index(g) + 1
            if isinstance(t, int) and t == TILES - 1 and not AHEAD_OF[g]:
                return len(FIRST) + GROUPS * t + LAST.index(g) + 1
            return GROUPS * (t - AHEAD_OF[g]) + (len(FIRST) + ORDER.index((AHEAD_OF[g], g)) + 1)

        def rank(kind, t, g):
            return len(kind) * t + (kind.index(g) + 1)

        def ring(parity, g, size):
            return (len(SPLIT) * parity + SPLIT.index(g)) % size

        def z_slot(parity, g):
            return Z_RING if g in FULL else ring(parity, g, Z_RING)

        def x_bank(t, g):
            order = FIRST.index(g) if isinstance(t, int) and t == 0 and AHEAD_OF[g] else (
                len(FIRST) + LAST.index(g) if isinstance(t, int) and t == TILES - 1 and not AHEAD_OF[g] else
                len(FIRST) + ORDER.index((AHEAD_OF[g], g)))
            return X_BANK + order % 2

        def reused(t, g, size):
            return not (isinstance(t, int) and t == 0 and SPLIT.index(g) < size)

        def makes(t, parity, s):
            return [(t + ahead, g, parity ^ ahead) for ahead, g in MAKES[s]
                    if not (ahead and isinstance(t, int) and t == TILES - 1)]

        def at_start(t):
            return isinstance(t, int) and t == 0

        def every_tile(eng, tile):
            tile(0, 0, True)
            with eng.Fori(0, (TILES - 4) // 2) as i:
                tile(2 * i + 1, 1, True)
                tile(2 * i + 2, 0, True)
            tile(TILES - 3, 1, True)
            tile(TILES - 2, 0, False)
            tile(TILES - 1, 1, False)

        def every_tile_by_block(eng, tile, between):
            tile(0, 0, True)
            with eng.Fori(0, BLOCKS - 1) as k:
                tile(T_BLOCK * k + 1, 1, True)
                tile(T_BLOCK * k + 2, 0, True)
                between(k + 1)
                with eng.Fori(0, 3) as i:
                    tile(T_BLOCK * k + 2 * i + 3, 1, True)
                    tile(T_BLOCK * k + 2 * i + 4, 0, True)
            with eng.Fori(0, 2) as i:
                tile(TILES - T_BLOCK + 2 * i + 1, 1, True)
                tile(TILES - T_BLOCK + 2 * i + 2, 0, True)
            tile(TILES - 3, 1, True)
            tile(TILES - 2, 0, False)
            tile(TILES - 1, 1, False)

        block = es.enter_context(nc.Block())

        @block.sync
        def _(sp):
            sp.dma_start(ids_sb[:], ids.rearrange("(k p) f -> p k f", p=P)).then_inc(ids_in, 16)
            sp.dma_start(z[0:XROWS, 2, 0:14 * P], selectors).then_inc(sel_in, 16)
            sp.dma_start(w0[:], filt0).then_inc(w0_in, 16)
            sp.dma_start(w0_t, filt0_t).then_inc(w0_in, 16)
            sp.dma_start(z[:, 0:2, :], filt1.rearrange("p (r c) -> p r c", r=2)).then_inc(w1_in, 16)
            for n, g in enumerate(FULL):
                sp.dma_start(w1_full[:, n, :, :].rearrange("p m n -> p (m n)"),
                             filt1[:, g * MG * N2:(g + 1) * MG * N2]).then_inc(small_in, 16)
            with nc.allow_non_contiguous_dma(reason="a few hundred bias and weight elements"):
                sp.dma_start(bias1[:], b_top1.rearrange("(c p) -> p c", p=P)).then_inc(small_in, 16)
                sp.dma_start(bias2[:], b_top2.rearrange("(c p) -> p c", p=P)).then_inc(small_in, 16)
                sp.dma_start(w3[:], w_top3.rearrange("(c p) o -> p (c o)", p=P)).then_inc(small_in, 16)

            def value(x):
                return x if isinstance(x, int) else sp.snap(x)

            def spread_parts(k):
                ready = value(k + 1)
                places = [value((k % 2) * (T_BLOCK * COLS) + q * 2 * COLS) for q in range(4)]
                sp.wait_ge(parts_ready, ready)
                for q, at in enumerate(places):
                    for part in range(PARTS):
                        sp.dma_start(xs[part * FIELDS:(part + 1) * FIELDS, bass.ds(at, 2 * COLS)],
                                     parts[q * 32:(q + 1) * 32, part, :, :, :].rearrange("p s d b -> p (s d b)")
                                     ).then_inc(xs_ready, 16)

            def turn_prev(t, parity):
                ready = value(t + 1)
                sp.wait_ge(relu1_done, ready)
                for turn in range(1, MG):
                    cut = P - turn * M_CHUNK
                    sp.dma_start(prev[0:cut, parity, turn, :],
                                 prev[turn * M_CHUNK:P, parity, 0, :]).then_inc(turned[parity], 16)
                    sp.dma_start(prev[cut:P, parity, turn, :],
                                 prev[0:turn * M_CHUNK, parity, 0, :]).then_inc(turned[parity], 16)

            spread_parts(0)
            turn_prev(0, 0)
            turn_prev(1, 1)

            def tile(t, parity, more):
                if not at_start(t) and not (isinstance(t, int) and t == TILES - 1):
                    turn_prev(t + 1, 1 - parity)

            every_tile_by_block(sp, tile, spread_parts)
            for g in SPLIT[-3:-1]:
                if g in ON_POOL:
                    sp.wait_ge(lo_pool, rank(ON_POOL, TILES - 1, g))
                else:
                    sp.wait_ge(lo_dve, rank(ON_DVE, TILES - 1, g))
            sp.dma_start(t1_w, w_top1[0:2 * P, :].rearrange("(k p) n -> p k n", p=P)).then_inc(tower_in, 16)
            sp.dma_start(t1_wc, w_top1[2 * P:2 * P + CTX, :]).then_inc(tower_in, 16)
            sp.dma_start(ctx_sb, ctx_t).then_inc(tower_in, 16)
            sp.dma_start(t2_w, w_top2.rearrange("(k p) n -> p k n", p=P)).then_inc(tower_in, 16)
            sp.wait_ge(t_act, 14)
            sp.dma_start(out.rearrange("b o -> o b"), y).then_inc(y_out, 16)
            sp.wait_ge(y_out, 16)

        @block.gpsimd
        def _(pool):
            def gather(k, fields, idx):
                for f in fields:
                    nc.gpsimd.indirect_dma_start(
                        emb[:, f, :], None, tables[f],
                        bass.IndirectOffsetOnAxis(idx[:, f:f + 1].bitcast(U32), 0)).then_inc(gathered, 16)

            pool.wait_ge(ids_in, 16)
            gather(0, range(FIELDS), ids_sb[:, 0, :])
            nc.gpsimd.tensor_copy(idx_now[:], ids_sb[:, 1, :]).then_inc(idx_ready, 1)
            pool.wait_ge(idx_ready, 1)
            pool.wait_ge(emb_taken, 1)
            gather(1, range(28), idx_now)

            def low_part(t, g, parity):
                if g not in ON_POOL:
                    return
                pool.wait_ge(hi_ready, rank(SPLIT, t, g))
                back, used = split_before(g, LO_RING)
                if reused(t, g, LO_RING):
                    pool.wait_ge(mm_done, groups_to(t + back, used))
                nc.gpsimd.tensor_tensor(z_lo[:, ring(parity, g, LO_RING), :], z[:, z_slot(parity, g), :],
                                        z_hi[:, ring(parity, g, HI_RING), :].bitcast(F32),
                                        ALU.subtract).then_inc(lo_pool, 1)

            for g in FIRST:
                low_part(0, g, 0)

            def tile(t, parity, k=None, fields=()):
                left = list(fields)
                for s in range(GROUPS):
                    for made in makes(t, parity, s):
                        low_part(*made)
                        if left and made[1] in ON_POOL:
                            gather(k, [left.pop(0)], idx_now)
                if left:
                    gather(k, left, idx_now)

            shares = [4, 4, 5, 5, 5, 5, 4, 0]
            by_tile = [range(sum(shares[:n]), sum(shares[:n + 1])) for n in range(T_BLOCK)]

            def half_before(k):
                for n in range(2):
                    tile(T_BLOCK * k + n + 1, (n + 1) % 2, k + 1, by_tile[6 + n])

            def half_after(k, more):
                if more:
                    pool.wait_ge(gathered, 16 * FIELDS * (k + 2))
                    nc.gpsimd.tensor_copy(idx_now[:], ids_sb[:, bass.ds(k + 2, 1), :].rearrange(
                        "p o f -> p (o f)")).then_inc(idx_ready, 1)
                    pool.wait_ge(idx_ready, k + 2)
                    pool.wait_ge(emb_taken, k + 2)
                for n in range(6):
                    tile(T_BLOCK * k + n + 3, (n + 1) % 2, k + 2, by_tile[n] if more else ())

            tile(0, 0)
            with pool.Fori(0, BLOCKS - 2) as k:
                half_before(k)
                half_after(k, True)
            half_before(BLOCKS - 2)
            half_after(BLOCKS - 2, False)
            with pool.Fori(0, (T_BLOCK - 2) // 2) as i:
                tile(TILES - T_BLOCK + 2 * i + 1, 1)
                tile(TILES - T_BLOCK + 2 * i + 2, 0)
            tile(TILES - 1, 1)

        @block.scalar
        def _(act):
            act.wait_ge(sel_in, 16)
            nc.scalar.activation(sel[:].rearrange("p k n -> p (k n)"), z[0:XROWS, 2, 0:14 * P],
                                 ACT.Copy).then_inc(sel_ready, 1)
            act.wait_ge(w0_ready, 1)
            nc.scalar.activation(w0_lhh[:], w0[0:96, SHIFTS, :], ACT.Copy).then_inc(w0_hi, 1)
            act.wait_ge(w1_in, 16)
            nc.scalar.activation(w1_hi[:].rearrange("p (r g) m n -> p r (g m n)", r=2), z[:, 0:2, :],
                                 ACT.Copy).then_inc(w1_hi_ready, 1)
            act.wait_ge(w1_hi_ready, 1)
            act.sem_inc(acc2_free, 2)

            def take_rep(t, first=False):
                act.wait_ge(s_ready, 4 * t + 1)
                if not first:
                    act.wait_ge(z1_ready, 3 * t)
                nc.scalar.activation(rep[:], ps[:, S_BANK, :], ACT.Copy).then_inc(rep_ready, 1)

            def relu1(t, parity, first=False):
                act.wait_ge(l1_done, t + 1)
                if not first:
                    act.wait_ge(z_ready, made_to(t - 2, LAST[-1]))
                    act.wait_ge(turned[parity], 16 * TURN_DMAS * (t // 2))
                    act.wait_ge(sum1_done, t - 1)
                nc.scalar.activation(prev[:, parity, 0, :], ps[:, ACC1 + parity, :], ACT.Relu).then_inc(relu1_done, 1)

            def relu2(t, parity):
                act.wait_ge(mm_done, GROUPS * (t + 1))
                act.wait_ge(cur2_free, t + 1)
                nc.scalar.activation(cur2[:].rearrange("p d b -> p (d b)"), ps[:, ACC2 + parity, :],
                                     ACT.Relu).then_inc(acc2_free, 1)

            def high_part(t, g, parity):
                if g not in SPLIT:
                    return
                act.wait_ge(z_ready, made_to(t, g))
                back, used = split_before(g, HI_RING)
                if reused(t, g, HI_RING):
                    act.wait_ge(mm_done, groups_to(t + back, used))
                nc.scalar.activation(z_hi[:, ring(parity, g, HI_RING), :], z[:, z_slot(parity, g), :],
                                     ACT.Copy).then_inc(hi_ready, 1)

            def high_half(t, first=False):
                act.wait_ge(z1_ready, 3 * t + 3)
                if not first:
                    act.wait_ge(l1_done, t)
                nc.scalar.activation(half_hl[:], z1_half[:], ACT.Copy).then_inc(half_hi, 1)

            for t in range(2):
                take_rep(t, t == 0)
                high_half(t, t == 0)
                relu1(t, t, True)
            for g in FIRST:
                high_part(0, g, 0)

            def tile(t, parity, more):
                for s in range(GROUPS):
                    if s == 0 and not at_start(t) and not (isinstance(t, int) and t == TILES - 1):
                        relu1(t + 1, 1 - parity)
                    if more and s == 0:
                        take_rep(t + 2)
                    if s == 1 and not at_start(t):
                        relu2(t - 1, 1 - parity)
                    for made in makes(t, parity, s):
                        high_part(*made)
                    if more and s == 4:
                        high_half(t + 2)

            every_tile(act, tile)
            relu2(TILES - 1, 1)

            act.wait_ge(small_in, 16 * (3 + len(FULL)))
            act.wait_ge(mm_done, GROUPS * TILES)
            for half in range(2):
                for o in range(4):
                    act.wait_ge(t_mm, 4 * half + o + 1)
                    nc.scalar.activation(z[:, 2 + half, o * COLS:(o + 1) * COLS], ps[:, 4 * half + o, :],
                                         ACT.Relu, bias=bias1[:, o:o + 1]).then_inc(t_act, 1)
            for half in range(2):
                for o in range(2):
                    act.wait_ge(t_mm, 8 + 2 * half + o + 1)
                    nc.scalar.activation(z1[:, 2 * half + o, :], ps[:, 2 * half + o, :],
                                         ACT.Relu, bias=bias2[:, o:o + 1]).then_inc(t_act, 1)
            for half in range(2):
                act.wait_ge(t_mm, 12 + half + 1)
                nc.scalar.activation(y[0:1, half * COLS:(half + 1) * COLS], ps[0:1, 4 + half, :],
                                     ACT.Copy).then_inc(t_act, 1)

        @block.vector
        def _(dve):
            steps = [0]

            def prepare(k):
                dve.wait_ge(gathered, 16 * FIELDS * (k + 1))
                nc.vector.transpose(emb_t[:], emb[:].rearrange("p h d -> p d h")).then_inc(emb_taken, 1)
                dve.wait_ge(emb_taken, k + 1)
                if not isinstance(k, int) or k:
                    dve.wait_ge(xs_ready, 16 * XS_DMAS * k)
                view = emb_t[:].rearrange("p d (s b) -> p s d b", s=2)
                for part in range(PARTS):
                    nc.vector.tensor_copy(parts[:, part, :, :, :], view).then_inc(
                        parts_ready if part == PARTS - 1 else prep_step, 1)
                    if part < PARTS - 1:
                        dve.wait_ge(prep_step, 4 * k + 2 * part + 1)
                        for s in range(2):
                            last = nc.vector.tensor_tensor(view[:, s, :, :], view[:, s, :, :],
                                                           parts[:, part, s, :, :], ALU.subtract)
                        last.then_inc(prep_step, 1)
                        dve.wait_ge(prep_step, 4 * k + 2 * part + 2)

            def z1_part(t, n, first=False):
                dve.wait_ge(s_ready, 4 * t + 2 + n)
                if n == 0:
                    dve.wait_ge(rep_ready, t + 1)
                    if not first:
                        dve.wait_ge(l1_done, t)
                if n < 2:
                    nc.vector.tensor_tensor(z1[:, 2 * n:2 * n + 2, :], ps[:, S_BANK:S_BANK + 2, :],
                                            rep[:, None, :].to_broadcast([P, 2, COLS]), ALU.mult).then_inc(z1_ready, 1)
                else:
                    nc.vector.tensor_tensor(z1_half[:], ps[0:96, S_BANK, :], rep[0:96, :],
                                            ALU.mult).then_inc(z1_ready, 1)

            def sum1(t, parity):
                dve.wait_ge(relu1_done, t + 1)
                nc.vector.tensor_reduce(sums[:, 0, bass.ds(B_TILE * t, B_TILE)],
                                        prev[:, parity, 0, :].rearrange("p (d b) -> p b d", d=DIM),
                                        AX.X, ALU.add).then_inc(sum1_done, 1)

            def sum2(t):
                dve.wait_ge(acc2_free, t + 3)
                nc.vector.tensor_reduce(sums[:, 1, bass.ds(B_TILE * t, B_TILE)],
                                        cur2[:].rearrange("p d b -> p b d"), AX.X, ALU.add).then_inc(cur2_free, 1)

            def product(t, g, parity):
                dve.wait_ge(x_ready, made_to(t, g))
                if g == FIRST[0]:
                    dve.wait_ge(turned[parity], 16 * TURN_DMAS * (t // 2 + 1))
                if g in FULL:
                    n = FULL.index(g) - 1
                    if n >= 0 or not at_start(t):
                        dve.wait_ge(mm_done, groups_to(t, FULL[n]) if n >= 0 else groups_to(t - 1, FULL[n]))
                elif reused(t, g, Z_RING):
                    back, used = split_before(g, Z_RING)
                    if used in ON_POOL:
                        dve.wait_ge(lo_pool, rank(ON_POOL, t + back, used))
                    else:
                        dve.wait_ge(lo_dve, rank(ON_DVE, t + back, used))
                nc.vector.tensor_tensor(z[:, z_slot(parity, g), :].rearrange("p (m c) -> p m c", m=MG),
                                        ps[:, x_bank(t, g), None, :].to_broadcast([P, MG, COLS]),
                                        prev[:, parity, :, :], ALU.mult).then_inc(z_ready, 1)

            def low_part(t, g, parity):
                if g not in ON_DVE:
                    return
                dve.wait_ge(hi_ready, rank(SPLIT, t, g))
                back, used = split_before(g, LO_RING)
                if reused(t, g, LO_RING):
                    dve.wait_ge(mm_done, groups_to(t + back, used))
                nc.vector.tensor_tensor(z_lo[:, ring(parity, g, LO_RING), :], z[:, z_slot(parity, g), :],
                                        z_hi[:, ring(parity, g, HI_RING), :].bitcast(F32),
                                        ALU.subtract).then_inc(lo_dve, 1)

            def low_half(t):
                dve.wait_ge(half_hi, t + 1)
                nc.vector.tensor_tensor(half_hl[64:96, :], z1_half[64:96, :], half_hl[64:96, :].bitcast(F32),
                                        ALU.subtract).then_inc(half_lo, 1)

            nc.vector.memset(cur2[:], 0.0).then_inc(cur2_free, 1)
            dve.wait_ge(w0_in, 32)
            nc.vector.tensor_tensor(w0[:], w0[:], w0_t, ALU.add).then_inc(w0_ready, 1)
            dve.wait_ge(w0_hi, 1)
            nc.vector.tensor_tensor(w0_lhh[0:32, :], w0[0:32, SHIFTS, :], w0_lhh[0:32, :].bitcast(F32),
                                    ALU.subtract).then_inc(w0_lo, 1)
            dve.wait_ge(w1_hi_ready, 1)
            nc.vector.tensor_tensor(w1_lo[:].rearrange("p (r g) m n -> p r (g m n)", r=2), z[:, 0:2, :],
                                    w1_hi[:].rearrange("p (r g) m n -> p r (g m n)", r=2).bitcast(F32),
                                    ALU.subtract).then_inc(w1_lo_ready, 1)
            dve.wait_ge(w1_lo_ready, 1)
            dve.wait_ge(sel_ready, 1)
            prepare(0)
            for t in range(2):
                for n in range(3):
                    z1_part(t, n, t == 0)
                low_half(t)
                if t == 0:
                    sum1(0, 0)

            def lows(pending, made):
                for one in pending:
                    low_part(*one)
                return [one for one in made if one[1] in ON_DVE]

            pending = []
            for g in FIRST:
                product(0, g, 0)
                pending = lows(pending, [(0, g, 0)])
            assert not pending

            def tile(t, parity, more):
                pending = []
                for s in range(GROUPS):
                    if more and 1 <= s <= 3:
                        z1_part(t + 2, s - 1)
                    if s == 2 and not (isinstance(t, int) and t == TILES - 1):
                        sum1(t + 1, 1 - parity)
                    if s == 4 and not at_start(t):
                        sum2(t - 1)
                    made = makes(t, parity, s)
                    for one in made:
                        product(*one)
                    if made:
                        pending = lows(pending, made)
                    if more and s == 6:
                        low_half(t + 2)
                lows(pending, [])

            every_tile_by_block(dve, tile, prepare)
            sum2(TILES - 1)

        @block.tensor
        def _(pe):
            def columns(t):
                return xs[:, bass.ds((t % (2 * T_BLOCK)) * COLS, COLS)]

            def spread(bank, form, t):
                return nc.tensor.matmul(ps[:, bank, :], sel[:, form, :], columns(t), start=True, stop=True)

            def l1_piece(t, n, first=False):
                if n == 0:
                    pe.wait_ge(xs_ready, 16 * XS_DMAS * (t // T_BLOCK + 1))
                    if not first:
                        pe.wait_ge(z1_ready, 3 * t)
                    spread(S_BANK, GROUPS, t).then_inc(s_ready, 1)
                elif n == 1:
                    pe.wait_ge(rep_ready, t + 1)
                    spread(S_BANK, GROUPS + 1, t)
                    spread(S_BANK + 1, GROUPS + 2, t).then_inc(s_ready, 1)
                elif n == 2:
                    pe.wait_ge(z1_ready, 3 * t + 1)
                    spread(S_BANK, GROUPS + 3, t)
                    spread(S_BANK + 1, GROUPS + 4, t).then_inc(s_ready, 1)
                else:
                    pe.wait_ge(z1_ready, 3 * t + 2)
                    spread(S_BANK, GROUPS + 5, t).then_inc(s_ready, 1)

            def l1_matmuls(t, parity, n, first=False):
                if n == 0:
                    pe.wait_ge(z1_ready, 3 * t + 2)
                    if not first:
                        pe.wait_ge(relu1_done, t - 1)
                acc = ps[:, ACC1 + parity, :]
                for s in (2 * n, 2 * n + 1):
                    nc.tensor.matmul(acc, w0[:, s, :], z1[:, s, :], start=(s == 0), stop=False)
                if n == 1:
                    pe.wait_ge(half_lo, t + 1)
                    nc.tensor.matmul(acc, w0_lhh[:], half_hl[:], start=False, stop=True).then_inc(l1_done, 1)

            def x_form(t, g, first=False):
                if not first:
                    pe.wait_ge(z_ready, made_to(t, g) - 2)
                spread(x_bank(t, g), g, t).then_inc(x_ready, 1)

            def group(t, g, parity):
                acc = ps[:, ACC2 + parity, :]
                if g in FULL:
                    pe.wait_ge(z_ready, made_to(t, g))
                    for m in range(MG):
                        last = nc.tensor.matmul(acc, w1_full[:, FULL.index(g), m, :],
                                                z[:, Z_RING, m * COLS:(m + 1) * COLS],
                                                start=(g == 0 and m == 0), stop=(g == GROUPS - 1 and m == MG - 1))
                else:
                    hi = z_hi[:, ring(parity, g, HI_RING), :]
                    lo = z_lo[:, ring(parity, g, LO_RING), :]
                    pe.wait_ge(hi_ready, rank(SPLIT, t, g))
                    for m in range(MG):
                        c = slice(m * COLS, (m + 1) * COLS)
                        nc.tensor.matmul(acc, w1_lo[:, g, m, :], hi[:, c], start=(g == 0 and m == 0), stop=False)
                        nc.tensor.matmul(acc, w1_hi[:, g, m, :], hi[:, c], start=False, stop=False)
                    if g in ON_POOL:
                        pe.wait_ge(lo_pool, rank(ON_POOL, t, g))
                    else:
                        pe.wait_ge(lo_dve, rank(ON_DVE, t, g))
                    for m in range(MG):
                        c = slice(m * COLS, (m + 1) * COLS)
                        last = nc.tensor.matmul(acc, w1_hi[:, g, m, :], lo[:, c], start=False,
                                                stop=(g == GROUPS - 1 and m == MG - 1))
                last.then_inc(mm_done, 1)

            pe.wait_ge(sel_ready, 1)
            pe.wait_ge(w0_ready, 1)
            pe.wait_ge(w0_lo, 1)
            for t in range(2):
                for n in range(4):
                    l1_piece(t, n, t == 0)
                l1_matmuls(t, t, 0, True)
                l1_matmuls(t, t, 1, True)
            for n, g in enumerate(FIRST):
                x_form(0, g, n < 2)
            pe.wait_ge(w1_lo_ready, 1)
            pe.wait_ge(small_in, 16 * (3 + len(FULL)))

            def tile(t, parity, more):
                pe.wait_ge(acc2_free, t + 1)
                for g in range(GROUPS):
                    if more and g < 4:
                        l1_piece(t + 2, g)
                    for made in makes(t, parity, g):
                        x_form(made[0], made[1])
                    group(t, g, parity)
                    if more and g in (4, 7):
                        l1_matmuls(t + 2, parity, (g - 4) // 3)

            every_tile(pe, tile)

            pe.wait_ge(tower_in, 64)
            pe.wait_ge(z_ready, GROUPS * TILES)
            for half in range(2):
                c = slice(half * COLS, (half + 1) * COLS)
                pe.wait_ge(cur2_free, TILES - 31 if half == 0 else TILES + 1)
                for o in range(4):
                    n = slice(o * P, (o + 1) * P)
                    acc = ps[:, 4 * half + o, :]
                    nc.tensor.matmul(acc, t1_wc[:, n], ctx_sb[:, c], start=True, stop=False)
                    nc.tensor.matmul(acc, t1_w[:, 0, n], sums[:, 0, c], start=False, stop=False)
                    nc.tensor.matmul(acc, t1_w[:, 1, n], sums[:, 1, c], start=False, stop=True).then_inc(t_mm, 1)
            for half in range(2):
                pe.wait_ge(t_act, 4 * (half + 1))
                for o in range(2):
                    for k in range(4):
                        last = nc.tensor.matmul(ps[:, 2 * half + o, :], t2_w[:, k, o * P:(o + 1) * P],
                                                z[:, 2 + half, k * COLS:(k + 1) * COLS], start=(k == 0), stop=(k == 3))
                    last.then_inc(t_mm, 1)
            for half in range(2):
                pe.wait_ge(t_act, 8 + 2 * (half + 1))
                for k in range(2):
                    last = nc.tensor.matmul(ps[0:1, 4 + half, :], w3[:, k:k + 1], z1[:, 2 * half + k, :],
                                            start=(k == 0), stop=(k == 1))
                last.then_inc(t_mm, 1)


def selector_matrix():
    import numpy as np
    sel = np.zeros((PARTS, FIELDS, 14, P), np.float32)
    for row in range(P):
        j, low = row // 32, row % 32
        for g in range(GROUPS):
            sel[:, H_CHUNK * g + j, g, row] = 1.0
        sel[:, low, GROUPS, row] = 1.0
        for s in range(SHIFTS):
            sel[:, (low + H_CHUNK * s + j) % FIELDS, GROUPS + 1 + s, row] = 1.0
        sel[:, (low + HALF) % FIELDS, GROUPS + 1 + SHIFTS, row] = 1.0
    return sel.reshape(XROWS, 14 * P)


def kernel(**inputs):
    import numpy as np
    import concourse.bacc as bacc
    from concourse.bass_utils import run_bass_kernel_spmd

    a = {name: np.ascontiguousarray(x) for name, x in inputs.items()}
    tables = [a[f"tbl_{f}"] for f in range(FIELDS)]
    w = a["L0_rec_filter_0"].reshape(FIELDS, FIELDS, N1)
    filt0 = np.zeros((P, SHIFTS + 1, N1), np.float32)
    filt0_t = np.zeros((P, SHIFTS + 1, N1), np.float32)
    for s in range(HALF + 1):
        for h in range(FIELDS if s < HALF else HALF):
            for copy in ((s % H_CHUNK,) if s < HALF else range(3)):
                row, chunk = copy * FIELDS + h, s // H_CHUNK
                filt0[row, chunk] = w[h, (h + s) % FIELDS]
                if s:
                    filt0_t[row, chunk] = w[(h + s) % FIELDS, h]
    v = a["L0_rec_filter_1"].reshape(GROUPS, H_CHUNK, MG, M_CHUNK, N2)
    filt1 = np.ascontiguousarray(np.stack([np.stack(
        [v[:, j, (j + turn) % MG] for turn in range(MG)], 1) for j in range(H_CHUNK)]).transpose(0, 3, 1, 2, 4))
    filt1 = filt1.reshape(P, GROUPS * MG * N2)
    arrays = {
        "ctx_t": np.ascontiguousarray(a["dense_ctx"].T), "ids_in_dram": a["ids"],
        "w_top1": a["W_top1"], "b_top1": a["b_top1"], "w_top2": a["W_top2"], "b_top2": a["b_top2"],
        "w_top3": a["W_top3"], "filt0": filt0, "filt0_t": filt0_t, "filt1": filt1,
        "selectors": selector_matrix(),
    }
    for f in range(FIELDS):
        arrays[f"table_{f}"] = tables[f]
    nc = bacc.Bacc("TRN2", target_bir_lowering=False, num_devices=1)
    d = {n: nc.dram_tensor(n, x.shape, mybir.dt.from_np(x.dtype), kind="ExternalInput").ap() for n, x in arrays.items()}
    out = nc.dram_tensor("y_dram", (BATCH, 1), F32, kind="ExternalOutput").ap()
    build_dlrm(nc, d["ctx_t"], d["ids_in_dram"], [d[f"table_{f}"] for f in range(FIELDS)], d["w_top1"], d["b_top1"],
               d["w_top2"], d["b_top2"], d["w_top3"], d["filt0"], d["filt0_t"], d["filt1"], d["selectors"], out)
    r = run_bass_kernel_spmd(nc, [arrays], core_ids=[0])
    return r.results[0]["y_dram"]
```

```python
from contextlib import ExitStack

import concourse.bass as bass
from concourse import mybir

F32 = mybir.dt.float32
F32R = mybir.dt.float32r
BF16 = mybir.dt.bfloat16
I32 = mybir.dt.int32
U32 = mybir.dt.uint32
ALU = mybir.AluOpType
ACT = mybir.ActivationFunctionType
AX = mybir.AxisListType

P = 128
FIELDS = 32
DIM = 32
BATCH = 1024
N1 = 128
N2 = 128
COLS = 512
B_TILE = COLS // DIM
TILES = BATCH // B_TILE
BLOCKS = BATCH // P
T_BLOCK = TILES // BLOCKS
PARTS = 3
XROWS = PARTS * FIELDS
H_CHUNK = 8
M_CHUNK = P // H_CHUNK
FORMS = FIELDS // H_CHUNK
TURNS = N1 // M_CHUNK
MG = TURNS // 2
GROUPS = 2 * FORMS
GCOLS = MG * COLS
S_CHUNK = P // FIELDS
SHIFTS = FIELDS // 2 // S_CHUNK
HALF = FIELDS // 2
Z1_SPLIT = 1

KINDS = "PFPPPPFV"
LEAD = {"P": 5, "V": 5, "F": 1}
FULL = [g for g in range(GROUPS) if KINDS[g] == "F"]
SPLIT = [g for g in range(GROUPS) if KINDS[g] != "F"]
ON_POOL = [g for g in range(GROUPS) if KINDS[g] == "P"]
ON_DVE = [g for g in range(GROUPS) if KINDS[g] == "V"]
Z_RING = 3
HI_RING = 4
LO_RING = 3
MAKES = [sorted(((s + LEAD[KINDS[g]]) // GROUPS, g) for g in range(GROUPS)
                if (s + LEAD[KINDS[g]]) % GROUPS == g) for s in range(GROUPS)]
L1_AT = (3, 7)
ORDER = [made for step in MAKES for made in step]
AHEAD_OF = {g: ahead for ahead, g in ORDER}
FIRST = [g for ahead, g in ORDER if ahead]
LAST = [g for ahead, g in ORDER if not ahead]
MADE = FIRST + LAST
PAIRS = [MADE[2 * f:2 * f + 2] for f in range(FORMS)]
FORM_OF = [MADE.index(g) // 2 for g in range(GROUPS)]
HALF_OF = [MADE.index(g) % 2 for g in range(GROUPS)]
FORMS_AT = {0: (0, 2), 1: (0, 3), 2: (1, 0), 6: (1, 1)}
SELECTORS = FORMS + 1 + SHIFTS + 1
assert len(FIRST) == 4 and not any(g in ON_DVE for _, g in MAKES[3])
assert [g for _, g in ORDER if g in SPLIT] == sorted(SPLIT, key=lambda g: (AHEAD_OF[g], g))

TOP1 = 512
TOP2 = 256
CTX = 16


def ring_slot(parity, g, size):
    return (len(SPLIT) * parity + SPLIT.index(g)) % size


def slot_before(parity, g, size):
    at = len(SPLIT) * parity + SPLIT.index(g)
    back = next(n for n in range(1, 2 * len(SPLIT) + 1) if (at - n) % (2 * len(SPLIT)) % size == at % size)
    r = SPLIT.index(g) - back
    return -(r // len(SPLIT)), SPLIT[r % len(SPLIT)]


LAST_IN = sorted((max(g for g in SPLIT if ring_slot((TILES - 1) % 2, g, Z_RING) == n), n) for n in range(Z_RING))
T1_SLOT, T2_SLOT, H_SLOT = (n for _, n in LAST_IN)


def build_dlrm(nc, ctx_t, ids, tables, w_top1, b_top1, w_top2, b_top2, w_top3, filt0, filt0_t, filt1, selectors, out):
    es = ExitStack()
    with es:
        def sb(name, shape, dt):
            return es.enter_context(nc.sbuf_tensor(name, shape, dt))

        def sem(name):
            return es.enter_context(nc.semaphore(name))

        idx_now = sb("idx_now", [P, FIELDS], I32)
        emb = sb("emb", [P, FIELDS, DIM], F32)
        emb_t = sb("emb_t", [P, DIM, 32], F32)
        part_now = sb("part_now", [P, 2, DIM, B_TILE], BF16)
        xs = sb("xs", [XROWS, 2 * T_BLOCK * COLS], BF16)
        sel = sb("sel", [XROWS, SELECTORS, P], BF16)
        rep = sb("rep", [P, COLS], F32)
        z1 = sb("z1", [P, MG, COLS], F32)
        half_hl = sb("half_hl", [3 * 32, COLS], F32R)
        w0_lhh = sb("w0_lhh", [3 * 32, N1], F32R)
        w0 = sb("w0", [P, SHIFTS - Z1_SPLIT, N1], F32)
        w0_hi = sb("w0_hi", [P, Z1_SPLIT, N1], F32R)
        w0_lo = sb("w0_lo", [P, Z1_SPLIT, N1], F32R)
        z1_hi = sb("z1_hi", [P, Z1_SPLIT, COLS], F32R)
        z1_lo = sb("z1_lo", [P, Z1_SPLIT, COLS], F32R)
        w1_hi = sb("w1_hi", [P, len(SPLIT), MG, N2], F32R)
        w1_lo = sb("w1_lo", [P, len(SPLIT), MG, N2], F32R)
        w1_full = sb("w1_full", [P, len(FULL), MG, N2], F32)
        prev = sb("prev", [P, 2, TURNS, COLS], F32)
        z = sb("z", [P, Z_RING + 1, GCOLS], F32)
        z_hi = sb("z_hi", [P, HI_RING, GCOLS], F32R)
        z_lo = sb("z_lo", [P, LO_RING, GCOLS], F32R)
        cur2 = sb("cur2", [P, DIM, B_TILE], F32)
        z1_half = cur2[0:3 * 32, :, :].rearrange("p d b -> p (d b)")
        sums = sb("sums", [P, 2, BATCH], F32)
        ids_sb = sums[:, 1, BATCH - BLOCKS * FIELDS:BATCH].bitcast(I32).rearrange("p (k f) -> p k f", k=BLOCKS)
        w1_in_ring = z[:].rearrange("p r c -> p (r c)")[:, 0:len(SPLIT) * MG * N2]
        bias1 = sb("bias1", [P, TOP1 // P], F32)
        bias2 = sb("bias2", [P, TOP2 // P], F32)
        w3 = sb("w3", [P, TOP2 // P], F32)
        w0_in_ring = z[:, Z_RING, 0:2 * (SHIFTS + 1) * N1].rearrange("p (h s n) -> p h s n", h=2, n=N1)
        first_parts = z[:, Z_RING, 0:PARTS * COLS].bitcast(BF16).rearrange(
            "p (r s d b) -> p r s d b", r=PARTS, s=2, d=DIM)
        t1_w = z[:, T1_SLOT, 0:2 * TOP1].rearrange("p (k n) -> p k n", k=2)
        ctx_in = z1[0:96, 0:2, :]
        wc_in = z1[0:96, 2, :]
        ctx_hhl = [z1_hi[0:96, 0, :], z1_lo[0:96, 0, :]]
        wc_lhh = half_hl
        t2_w = z[:, T2_SLOT, 0:4 * TOP2].rearrange("p (k n) -> p k n", k=4)
        hidden = [z[:, H_SLOT, :], z[:, Z_RING, :]]
        emb_tiles = emb_t[:].rearrange("p d (s b) -> p s d b", s=2)
        y = emb_t[0:1, :, :].rearrange("p d b -> p (d b)")
        ps = es.enter_context(nc.psum_tensor("ps", [P, 8, COLS], F32))
        X_BANK, S_BANK, ACC1, ACC2 = 0, 2, 4, 6

        ids_in = sem("ids_in")
        w0_in = sem("w0_in")
        w1_in = sem("w1_in")
        sel_in = sem("sel_in")
        small_in = sem("small_in")
        tower_in = sem("tower_in")
        ctx_clear = sem("ctx_clear")
        ctx_loaded = sem("ctx_loaded")
        ctx_hi = sem("ctx_hi")
        ctx_lo = sem("ctx_lo")
        idx_ready = sem("idx_ready")
        gathered = sem("gathered")
        emb_taken = sem("emb_taken")
        part_ready = sem("part_ready")
        rest_ready = sem("rest_ready")
        xs_first = sem("xs_first")
        xs_ready = sem("xs_ready")
        sel_ready = sem("sel_ready")
        w0_ready = sem("w0_ready")
        w1_hi_ready = sem("w1_hi_ready")
        w1_lo_ready = sem("w1_lo_ready")
        s_ready = sem("s_ready")
        rep_ready = sem("rep_ready")
        z1_ready = sem("z1_ready")
        half_hi = sem("half_hi")
        half_lo = sem("half_lo")
        z1_hi_ready = sem("z1_hi_ready")
        z1_lo_ready = sem("z1_lo_ready")
        w0_hi_ready = sem("w0_hi_ready")
        w0_lo_ready = sem("w0_lo_ready")
        l1_done = sem("l1_done")
        relu1_done = sem("relu1_done")
        sum1_done = sem("sum1_done")
        turned = [[sem(f"turned_{half}_{x}") for half in ("low", "high")] for x in ("even", "odd")]
        x_ready = sem("x_ready")
        z_ready = sem("z_ready")
        hi_ready = sem("hi_ready")
        lo_pool = sem("lo_pool")
        lo_dve = sem("lo_dve")
        mm_done = sem("mm_done")
        acc2_free = sem("acc2_free")
        cur2_free = sem("cur2_free")
        t_mm = sem("t_mm")
        t_act = sem("t_act")
        y_out = sem("y_out")

        TURN_DMAS = (2 * (MG - 1), 2 * (TURNS - MG))
        XS_DMAS = 4 * PARTS

        def spread_to(k):
            return 16 * XS_DMAS * k + 16 * (XS_DMAS - PARTS)

        def part_to(k, part):
            return PARTS * k + (part + 1)

        def groups_to(t, g):
            return GROUPS * t + (g + 1)

        def made_to(t, g):
            if isinstance(t, int) and t == 0 and AHEAD_OF[g]:
                return FIRST.index(g) + 1
            if isinstance(t, int) and t == TILES - 1 and not AHEAD_OF[g]:
                return len(FIRST) + GROUPS * t + LAST.index(g) + 1
            return GROUPS * (t - AHEAD_OF[g]) + (len(FIRST) + ORDER.index((AHEAD_OF[g], g)) + 1)

        def rank(kind, t, g):
            return len(kind) * t + (kind.index(g) + 1)

        def z_slot(parity, g):
            return Z_RING if g in FULL else ring_slot(parity, g, Z_RING)

        def form_to(t, f):
            return FORMS * t + (f + 1)

        def reused(t, g, size):
            return not (isinstance(t, int) and slot_before(t % 2, g, size)[0] > t)

        def makes(t, parity, s):
            return [(t + ahead, g, parity ^ ahead) for ahead, g in MAKES[s]
                    if not (ahead and isinstance(t, int) and t == TILES - 1)]

        def at_start(t):
            return isinstance(t, int) and t == 0

        def every_tile(eng, tile):
            tile(0, 0, True)
            with eng.Fori(0, (TILES - 4) // 2) as i:
                tile(2 * i + 1, 1, True)
                tile(2 * i + 2, 0, True)
            tile(TILES - 3, 1, True)
            tile(TILES - 2, 0, False)
            tile(TILES - 1, 1, False)

        def every_tile_by_block(eng, tile):
            tile(0, 0, True)
            with eng.Fori(0, BLOCKS - 1) as k:
                tile(T_BLOCK * k + 1, 1, True)
                for part in range(PARTS):
                    tile(T_BLOCK * k + 2 + part, part % 2, True, k + 1, part)
                with eng.Fori(0, 2) as i:
                    tile(T_BLOCK * k + 2 * i + 5, 1, True)
                    tile(T_BLOCK * k + 2 * i + 6, 0, True)
            with eng.Fori(0, 2) as i:
                tile(TILES - T_BLOCK + 2 * i + 1, 1, True)
                tile(TILES - T_BLOCK + 2 * i + 2, 0, True)
            tile(TILES - 3, 1, True)
            tile(TILES - 2, 0, False)
            tile(TILES - 1, 1, False)

        block = es.enter_context(nc.Block())

        @block.sync
        def _(sp):
            sp.dma_start(ids_sb, ids.rearrange("(k p) f -> p k f", p=P)).then_inc(ids_in, 16)
            sp.dma_start(z[0:XROWS, 2, 0:SELECTORS * P], selectors).then_inc(sel_in, 16)
            sp.dma_start(w0_in_ring[:, 0, :, :], filt0).then_inc(w0_in, 16)
            sp.dma_start(w0_in_ring[:, 1, :, :], filt0_t).then_inc(w0_in, 16)
            sp.dma_start(w1_in_ring, filt1[:, 0:len(SPLIT) * MG * N2]).then_inc(w1_in, 16)
            for n in range(len(FULL)):
                sp.dma_start(w1_full[:, n, :, :].rearrange("p m n -> p (m n)"),
                             filt1[:, (len(SPLIT) + n) * MG * N2:(len(SPLIT) + n + 1) * MG * N2]).then_inc(small_in, 16)
            with nc.allow_non_contiguous_dma(reason="a few hundred bias and weight elements"):
                sp.dma_start(bias1[:], b_top1.rearrange("(c p) -> p c", p=P)).then_inc(small_in, 16)
                sp.dma_start(bias2[:], b_top2.rearrange("(c p) -> p c", p=P)).then_inc(small_in, 16)
                sp.dma_start(w3[:], w_top3.rearrange("(c p) o -> p (c o)", p=P)).then_inc(small_in, 16)

            def value(x):
                return x if isinstance(x, int) else sp.snap(x)

            def spread_first():
                for q in range(4):
                    for part in range(PARTS):
                        if q == 0:
                            sp.wait_ge(part_ready, part_to(0, part))
                        sp.dma_start(xs[part * FIELDS:(part + 1) * FIELDS, q * 2 * COLS:(q + 1) * 2 * COLS],
                                     first_parts[q * 32:(q + 1) * 32, part, :, :, :].rearrange(
                                         "p s d b -> p (s d b)")).then_inc(xs_first if q == 0 else xs_ready, 16)

            def spread_part(k, part):
                ready = value(part_to(k, part))
                places = [value((k % 2) * (T_BLOCK * COLS) + q * 2 * COLS) for q in range(4)]
                sp.wait_ge(part_ready, ready)
                for q, at in enumerate(places):
                    sp.dma_start(xs[part * FIELDS:(part + 1) * FIELDS, bass.ds(at, 2 * COLS)],
                                 part_now[q * 32:(q + 1) * 32, :, :, :].rearrange("p s d b -> p (s d b)")
                                 ).then_inc(xs_ready, 16)

            def turn_prev(t, parity):
                ready = value(t + 1)
                sp.wait_ge(relu1_done, ready)
                for turn in range(1, TURNS):
                    cut = P - turn * M_CHUNK
                    done = turned[parity][turn // MG]
                    sp.dma_start(prev[0:cut, parity, turn, :],
                                 prev[turn * M_CHUNK:P, parity, 0, :]).then_inc(done, 16)
                    sp.dma_start(prev[cut:P, parity, turn, :],
                                 prev[0:turn * M_CHUNK, parity, 0, :]).then_inc(done, 16)

            spread_first()
            turn_prev(0, 0)
            turn_prev(1, 1)

            def tile(t, parity, more, block=None, part=None):
                if not at_start(t) and not (isinstance(t, int) and t == TILES - 1):
                    turn_prev(t + 1, 1 - parity)
                if block is not None:
                    spread_part(block, part)

            every_tile_by_block(sp, tile)
            sp.wait_ge(ctx_clear, 1)
            for copy in range(3):
                rows = slice(32 * copy, 32 * copy + CTX)
                sp.dma_start(ctx_in[rows, :, :], ctx_t.rearrange("c (h b) -> c h b", h=2)).then_inc(ctx_loaded, 16)
                sp.dma_start(wc_in[rows, :], w_top1[2 * P:2 * P + CTX, :]).then_inc(ctx_loaded, 16)
            for g, _ in LAST_IN[:2]:
                if g in ON_POOL:
                    sp.wait_ge(lo_pool, rank(ON_POOL, TILES - 1, g))
                else:
                    sp.wait_ge(lo_dve, rank(ON_DVE, TILES - 1, g))
            sp.dma_start(t1_w, w_top1[0:2 * P, :].rearrange("(k p) n -> p k n", p=P)).then_inc(tower_in, 16)
            sp.dma_start(t2_w, w_top2.rearrange("(k p) n -> p k n", p=P)).then_inc(tower_in, 16)
            sp.wait_ge(t_act, 14)
            sp.dma_start(out.rearrange("b o -> o b"), y).then_inc(y_out, 16)
            sp.wait_ge(y_out, 16)

        @block.gpsimd
        def _(pool):
            def gather(k, fields, idx):
                for f in fields:
                    nc.gpsimd.indirect_dma_start(
                        emb[:, f, :], None, tables[f],
                        bass.IndirectOffsetOnAxis(idx[:, f:f + 1].bitcast(U32), 0)).then_inc(gathered, 16)

            pool.wait_ge(ids_in, 16)
            gather(0, range(FIELDS), ids_sb[:, 0, :])
            nc.gpsimd.tensor_copy(idx_now[:], ids_sb[:, 1, :]).then_inc(idx_ready, 1)
            pool.wait_ge(idx_ready, 1)
            pool.wait_ge(emb_taken, 1)
            gather(1, range(29), idx_now)

            def low_part(t, g, parity):
                if g not in ON_POOL:
                    return
                pool.wait_ge(hi_ready, rank(SPLIT, t, g))
                back, used = slot_before(parity, g, LO_RING)
                if reused(t, g, LO_RING):
                    pool.wait_ge(mm_done, groups_to(t - back, used))
                nc.gpsimd.tensor_tensor(z_lo[:, ring_slot(parity, g, LO_RING), :], z[:, z_slot(parity, g), :],
                                        z_hi[:, ring_slot(parity, g, HI_RING), :].bitcast(F32),
                                        ALU.subtract).then_inc(lo_pool, 1)

            for g in FIRST:
                low_part(0, g, 0)

            def tile(t, parity, k=None, fields=()):
                left = list(fields)
                for s in range(GROUPS):
                    for made in makes(t, parity, s):
                        low_part(*made)
                        if left and made[1] in ON_POOL:
                            gather(k, [left.pop(0)], idx_now)
                if left:
                    gather(k, left, idx_now)

            shares = [5, 5, 5, 5, 5, 4, 3, 0]
            by_tile = [range(sum(shares[:n]), sum(shares[:n + 1])) for n in range(T_BLOCK)]

            def half_before(k):
                for n in range(2):
                    tile(T_BLOCK * k + n + 1, (n + 1) % 2, k + 1, by_tile[6 + n])

            def half_after(k, more):
                if more:
                    pool.wait_ge(gathered, 16 * FIELDS * (k + 2))
                    nc.gpsimd.tensor_copy(idx_now[:], ids_sb[:, bass.ds(k + 2, 1), :].rearrange(
                        "p o f -> p (o f)")).then_inc(idx_ready, 1)
                    pool.wait_ge(idx_ready, k + 2)
                    pool.wait_ge(emb_taken, k + 2)
                for n in range(6):
                    tile(T_BLOCK * k + n + 3, (n + 1) % 2, k + 2, by_tile[n] if more else ())

            tile(0, 0)
            with pool.Fori(0, BLOCKS - 2) as k:
                half_before(k)
                half_after(k, True)
            half_before(BLOCKS - 2)
            half_after(BLOCKS - 2, False)
            with pool.Fori(0, (T_BLOCK - 2) // 2) as i:
                tile(TILES - T_BLOCK + 2 * i + 1, 1)
                tile(TILES - T_BLOCK + 2 * i + 2, 0)
            tile(TILES - 1, 1)

        @block.scalar
        def _(act):
            act.wait_ge(sel_in, 16)
            nc.scalar.activation(sel[:].rearrange("p k n -> p (k n)"), z[0:XROWS, 2, 0:SELECTORS * P],
                                 ACT.Copy).then_inc(sel_ready, 1)
            act.wait_ge(w0_ready, 1)
            nc.scalar.activation(w0_lhh[:], w0_in_ring[0:96, 0, SHIFTS, :], ACT.Copy).then_inc(w0_hi_ready, 1)
            nc.scalar.activation(w0_hi[:], w0_in_ring[:, 0, 0:Z1_SPLIT, :], ACT.Copy).then_inc(w0_hi_ready, 1)
            act.wait_ge(w1_in, 16)
            nc.scalar.activation(w1_hi[:].rearrange("p g m n -> p (g m n)"), w1_in_ring,
                                 ACT.Copy).then_inc(w1_hi_ready, 1)
            act.wait_ge(w1_hi_ready, 1)
            act.sem_inc(acc2_free, 2)

            def take_rep(t, first=False):
                act.wait_ge(s_ready, 4 * t + 1)
                if not first:
                    act.wait_ge(z1_ready, 3 * t)
                nc.scalar.activation(rep[:], ps[:, S_BANK, :], ACT.Copy).then_inc(rep_ready, 1)

            def relu1(t, parity, first=False):
                act.wait_ge(l1_done, t + 1)
                if not first:
                    act.wait_ge(z_ready, made_to(t - 2, LAST[-1]))
                    for half in range(2):
                        act.wait_ge(turned[parity][half], 16 * TURN_DMAS[half] * (t // 2))
                    act.wait_ge(sum1_done, t - 1)
                nc.scalar.activation(prev[:, parity, 0, :], ps[:, ACC1 + parity, :], ACT.Relu).then_inc(relu1_done, 1)

            def relu2(t, parity):
                act.wait_ge(mm_done, GROUPS * (t + 1))
                act.wait_ge(cur2_free, t + 1)
                if not (isinstance(t, int) and t >= TILES - 2):
                    act.wait_ge(half_lo, t + 3)
                nc.scalar.activation(cur2[:].rearrange("p d b -> p (d b)"), ps[:, ACC2 + parity, :],
                                     ACT.Relu).then_inc(acc2_free, 1)

            def high_part(t, g, parity):
                if g not in SPLIT:
                    return
                act.wait_ge(z_ready, made_to(t, g))
                back, used = slot_before(parity, g, HI_RING)
                if reused(t, g, HI_RING):
                    act.wait_ge(mm_done, groups_to(t - back, used))
                nc.scalar.activation(z_hi[:, ring_slot(parity, g, HI_RING), :], z[:, z_slot(parity, g), :],
                                     ACT.Copy).then_inc(hi_ready, 1)

            def high_half(t, first=False):
                act.wait_ge(z1_ready, 3 * t + 3)
                if not first:
                    act.wait_ge(l1_done, t)
                nc.scalar.activation(half_hl[:], z1_half, ACT.Copy).then_inc(half_hi, 1)

            def high_first(t):
                act.wait_ge(z1_ready, 3 * t + 1)
                nc.scalar.activation(z1_hi[:], z1[:, 0:Z1_SPLIT, :], ACT.Copy).then_inc(z1_hi_ready, 1)

            def cast_part(k, part):
                if part == 0:
                    act.wait_ge(emb_taken, k + 1)
                else:
                    act.wait_ge(rest_ready, 2 * k + part)
                if isinstance(k, int):
                    place = first_parts[:, part, :, :, :]
                else:
                    act.wait_ge(xs_ready, spread_to(k - 1) + 64 * part)
                    place = part_now[:]
                nc.scalar.activation(place, emb_tiles, ACT.Copy).then_inc(part_ready, 1)

            for part in range(PARTS):
                cast_part(0, part)
            for t in range(2):
                take_rep(t, t == 0)
                high_first(t)
                if t == 1:
                    high_part(0, FIRST[0], 0)
                high_half(t, t == 0)
                relu1(t, t, True)
            for g in FIRST[1:]:
                high_part(0, g, 0)

            def tile(t, parity, more, block=None, part=None):
                for s in range(GROUPS):
                    if block is not None and s == 3:
                        cast_part(block, part)
                    if s == 0 and not at_start(t) and not (isinstance(t, int) and t == TILES - 1):
                        relu1(t + 1, 1 - parity)
                    if more and s == 0:
                        take_rep(t + 2)
                    if s == 1 and not at_start(t):
                        relu2(t - 1, 1 - parity)
                    for made in makes(t, parity, s):
                        high_part(*made)
                    if more and s == 1:
                        high_first(t + 2)
                    if more and s == 4:
                        high_half(t + 2)

            every_tile_by_block(act, tile)
            act.wait_ge(ctx_loaded, 16 * 6)
            for half in range(2):
                nc.scalar.activation(ctx_hhl[half], ctx_in[:, half, :], ACT.Copy).then_inc(ctx_hi, 1)
            nc.scalar.activation(wc_lhh[:], wc_in, ACT.Copy).then_inc(ctx_hi, 1)
            relu2(TILES - 1, 1)

            act.wait_ge(small_in, 16 * (3 + len(FULL)))
            act.wait_ge(mm_done, GROUPS * TILES)
            for half in range(2):
                for o in range(4):
                    act.wait_ge(t_mm, 4 * half + o + 1)
                    nc.scalar.activation(hidden[half][:, o * COLS:(o + 1) * COLS], ps[:, 4 * half + o, :],
                                         ACT.Relu, bias=bias1[:, o:o + 1]).then_inc(t_act, 1)
            for half in range(2):
                for o in range(2):
                    act.wait_ge(t_mm, 8 + 2 * half + o + 1)
                    nc.scalar.activation(z1[:, 2 * half + o, :], ps[:, 2 * half + o, :],
                                         ACT.Relu, bias=bias2[:, o:o + 1]).then_inc(t_act, 1)
            for half in range(2):
                act.wait_ge(t_mm, 12 + half + 1)
                nc.scalar.activation(y[0:1, half * COLS:(half + 1) * COLS], ps[0:1, 4 + half, :],
                                     ACT.Copy).then_inc(t_act, 1)

        @block.vector
        def _(dve):
            def take_emb(k):
                dve.wait_ge(gathered, 16 * FIELDS * (k + 1))
                if not isinstance(k, int):
                    dve.wait_ge(part_ready, part_to(k - 1, PARTS - 1))
                nc.vector.transpose(emb_t[:], emb[:].rearrange("p h d -> p d h")).then_inc(emb_taken, 1)

            def take_rest(k, part):
                dve.wait_ge(part_ready, part_to(k, part))
                place = first_parts[:, part, :, :, :] if isinstance(k, int) else part_now[:]
                nc.vector.tensor_tensor(emb_tiles, emb_tiles, place,
                                        ALU.subtract).then_inc(rest_ready, 1)

            def z1_part(t, n, first=False):
                dve.wait_ge(s_ready, 4 * t + 2 + n)
                if n == 0:
                    dve.wait_ge(rep_ready, t + 1)
                    if not first:
                        dve.wait_ge(l1_done, t)
                if n < 2:
                    nc.vector.tensor_tensor(z1[:, 2 * n:2 * n + 2, :], ps[:, S_BANK:S_BANK + 2, :],
                                            rep[:, None, :].to_broadcast([P, 2, COLS]), ALU.mult).then_inc(z1_ready, 1)
                else:
                    dve.wait_ge(cur2_free, 1 if isinstance(t, int) and t < 2 else t - 1)
                    nc.vector.tensor_tensor(z1_half, ps[0:96, S_BANK, :], rep[0:96, :],
                                            ALU.mult).then_inc(z1_ready, 1)

            def sum1(t, parity):
                dve.wait_ge(relu1_done, t + 1)
                nc.vector.tensor_reduce(sums[:, 0, bass.ds(B_TILE * t, B_TILE)],
                                        prev[:, parity, 0, :].rearrange("p (d b) -> p b d", d=DIM),
                                        AX.X, ALU.add).then_inc(sum1_done, 1)

            def sum2(t):
                dve.wait_ge(acc2_free, t + 3)
                nc.vector.tensor_reduce(sums[:, 1, bass.ds(B_TILE * t, B_TILE)],
                                        cur2[:].rearrange("p d b -> p b d"), AX.X, ALU.add).then_inc(cur2_free, 1)

            def product(t, g, parity):
                half = HALF_OF[g]
                dve.wait_ge(x_ready, form_to(t, FORM_OF[g]))
                if g in FIRST[:2]:
                    dve.wait_ge(turned[parity][half], 16 * TURN_DMAS[half] * (t // 2 + 1))
                if g in FULL:
                    n = FULL.index(g) - 1
                    if n >= 0 or not at_start(t):
                        dve.wait_ge(mm_done, groups_to(t, FULL[n]) if n >= 0 else groups_to(t - 1, FULL[n]))
                elif reused(t, g, Z_RING):
                    back, used = slot_before(parity, g, Z_RING)
                    if used in ON_POOL:
                        dve.wait_ge(lo_pool, rank(ON_POOL, t - back, used))
                    else:
                        dve.wait_ge(lo_dve, rank(ON_DVE, t - back, used))
                nc.vector.tensor_tensor(z[:, z_slot(parity, g), :].rearrange("p (m c) -> p m c", m=MG),
                                        ps[:, X_BANK + FORM_OF[g] % 2, None, :].to_broadcast([P, MG, COLS]),
                                        prev[:, parity, half * MG:(half + 1) * MG, :], ALU.mult).then_inc(z_ready, 1)

            def low_part(t, g, parity):
                if g not in ON_DVE:
                    return
                dve.wait_ge(hi_ready, rank(SPLIT, t, g))
                back, used = slot_before(parity, g, LO_RING)
                if reused(t, g, LO_RING):
                    dve.wait_ge(mm_done, groups_to(t - back, used))
                nc.vector.tensor_tensor(z_lo[:, ring_slot(parity, g, LO_RING), :], z[:, z_slot(parity, g), :],
                                        z_hi[:, ring_slot(parity, g, HI_RING), :].bitcast(F32),
                                        ALU.subtract).then_inc(lo_dve, 1)

            def low_first(t):
                dve.wait_ge(z1_hi_ready, t + 1)
                nc.vector.tensor_tensor(z1_lo[:], z1[:, 0:Z1_SPLIT, :],
                                        z1_hi[:].bitcast(F32), ALU.subtract).then_inc(z1_lo_ready, 1)

            def low_half(t):
                dve.wait_ge(half_hi, t + 1)
                nc.vector.tensor_tensor(half_hl[64:96, :], z1_half[64:96, :], half_hl[64:96, :].bitcast(F32),
                                        ALU.subtract).then_inc(half_lo, 1)

            nc.vector.memset(cur2[:], 0.0).then_inc(cur2_free, 1)
            dve.wait_ge(w0_in, 32)
            w0_sum = w0_in_ring[:, 0, :, :]
            nc.vector.tensor_tensor(w0_sum, w0_sum, w0_in_ring[:, 1, :, :], ALU.add).then_inc(w0_ready, 1)
            dve.wait_ge(w0_ready, 1)
            nc.vector.tensor_copy(w0[:], w0_sum[:, Z1_SPLIT:SHIFTS, :]).then_inc(w0_lo_ready, 1)
            dve.wait_ge(w0_hi_ready, 2)
            nc.vector.tensor_tensor(w0_lhh[0:32, :], w0_sum[0:32, SHIFTS, :], w0_lhh[0:32, :].bitcast(F32),
                                    ALU.subtract).then_inc(w0_lo_ready, 1)
            nc.vector.tensor_tensor(w0_lo[:], w0_sum[:, 0:Z1_SPLIT, :], w0_hi[:].bitcast(F32),
                                    ALU.subtract).then_inc(w0_lo_ready, 1)
            dve.wait_ge(w0_lo_ready, 3)
            dve.wait_ge(w1_hi_ready, 1)
            nc.vector.tensor_tensor(w1_lo[:].rearrange("p g m n -> p (g m n)"), w1_in_ring,
                                    w1_hi[:].rearrange("p g m n -> p (g m n)").bitcast(F32),
                                    ALU.subtract).then_inc(w1_lo_ready, 1)
            dve.wait_ge(w1_lo_ready, 1)
            dve.wait_ge(sel_ready, 1)
            take_emb(0)
            take_rest(0, 0)
            take_rest(0, 1)
            for t in range(2):
                for n in range(3):
                    if t == 1 and n == 2:
                        product(0, FIRST[0], 0)
                    z1_part(t, n, t == 0)
                    if n == 1:
                        low_first(t)
                low_half(t)
                if t == 0:
                    sum1(0, 0)

            def lows(pending, made):
                for one in pending:
                    low_part(*one)
                return [one for one in made if one[1] in ON_DVE]

            assert all(g in ON_POOL for g in FIRST)
            dve.wait_ge(xs_ready, spread_to(0))
            for g in FIRST[1:]:
                product(0, g, 0)

            def tile(t, parity, more, block=None, part=None):
                pending = []
                if isinstance(t, int) and t == TILES - 1:
                    dve.wait_ge(l1_done, TILES)
                    nc.vector.memset(z1[0:96, 0:3, :], 0.0).then_inc(ctx_clear, 1)
                for s in range(GROUPS):
                    if block is not None and s == 2:
                        take_emb(block) if part == 0 else take_rest(block, part - 1)
                    if s == 2 and not (isinstance(t, int) and t == TILES - 1):
                        sum1(t + 1, 1 - parity)
                    if more and s == 1:
                        z1_part(t + 2, 0)
                    if more and s == 2:
                        z1_part(t + 2, 1)
                        low_first(t + 2)
                    if s == 3 and not at_start(t):
                        sum2(t - 1)
                    made = makes(t, parity, s)
                    for one in made:
                        product(*one)
                    if more and s == 3:
                        z1_part(t + 2, 2)
                    if made and s != 3:
                        pending = lows(pending, made)
                    if more and s == 5:
                        low_half(t + 2)
                lows(pending, [])

            every_tile_by_block(dve, tile)
            dve.wait_ge(ctx_hi, 3)
            for half in range(2):
                nc.vector.tensor_tensor(ctx_hhl[half][64:96, :], ctx_in[64:96, half, :],
                                        ctx_hhl[half][64:96, :].bitcast(F32), ALU.subtract).then_inc(ctx_lo, 1)
            nc.vector.tensor_tensor(wc_lhh[0:32, :], wc_in[0:32, :], wc_lhh[0:32, :].bitcast(F32),
                                    ALU.subtract).then_inc(ctx_lo, 1)
            sum2(TILES - 1)

        @block.tensor
        def _(pe):
            def columns(t):
                return xs[:, bass.ds((t % (2 * T_BLOCK)) * COLS, COLS)]

            def spread(bank, form, t):
                return nc.tensor.matmul(ps[:, bank, :], sel[:, form, :], columns(t), start=True, stop=True)

            def l1_piece(t, n, first=False):
                if n == 0:
                    if isinstance(t, int) and t < 2:
                        pe.wait_ge(xs_first, 16 * PARTS)
                    else:
                        pe.wait_ge(xs_ready, spread_to(t // T_BLOCK))
                    if not first:
                        pe.wait_ge(z1_ready, 3 * t)
                    spread(S_BANK, FORMS, t).then_inc(s_ready, 1)
                elif n == 1:
                    pe.wait_ge(rep_ready, t + 1)
                    spread(S_BANK, FORMS + 1, t)
                    spread(S_BANK + 1, FORMS + 2, t).then_inc(s_ready, 1)
                elif n == 2:
                    pe.wait_ge(z1_ready, 3 * t + 1)
                    spread(S_BANK, FORMS + 3, t)
                    spread(S_BANK + 1, FORMS + 4, t).then_inc(s_ready, 1)
                else:
                    pe.wait_ge(z1_ready, 3 * t + 2)
                    spread(S_BANK, FORMS + 5, t).then_inc(s_ready, 1)

            def l1_matmuls(t, parity, n, first=False):
                if n == 0:
                    pe.wait_ge(z1_ready, 3 * t + 2)
                    if not first:
                        pe.wait_ge(relu1_done, t - 1)
                acc = ps[:, ACC1 + parity, :]
                for s in range(max(2 * n, Z1_SPLIT), 2 * n + 2):
                    nc.tensor.matmul(acc, w0[:, s - Z1_SPLIT, :], z1[:, s, :], start=(s == Z1_SPLIT), stop=False)
                if n == 0:
                    pe.wait_ge(z1_lo_ready, t + 1)
                    for s in range(Z1_SPLIT):
                        nc.tensor.matmul(acc, w0_lo[:, s, :], z1_hi[:, s, :], start=False, stop=False)
                        nc.tensor.matmul(acc, w0_hi[:, s, :], z1_hi[:, s, :], start=False, stop=False)
                        nc.tensor.matmul(acc, w0_hi[:, s, :], z1_lo[:, s, :], start=False, stop=False)
                if n == 1:
                    pe.wait_ge(half_lo, t + 1)
                    nc.tensor.matmul(acc, w0_lhh[:], half_hl[:], start=False, stop=True).then_inc(l1_done, 1)

            def x_form(t, f):
                if f >= 2:
                    pe.wait_ge(z_ready, made_to(t, PAIRS[f - 2][1]))
                elif not at_start(t):
                    pe.wait_ge(z_ready, made_to(t - 1, PAIRS[f + 2][1]))
                spread(X_BANK + f % 2, f, t).then_inc(x_ready, 1)

            def group(t, g, parity):
                acc = ps[:, ACC2 + parity, :]
                if g in FULL:
                    pe.wait_ge(z_ready, made_to(t, g))
                    for m in range(MG):
                        last = nc.tensor.matmul(acc, w1_full[:, FULL.index(g), m, :],
                                                z[:, Z_RING, m * COLS:(m + 1) * COLS],
                                                start=(g == 0 and m == 0), stop=(g == GROUPS - 1 and m == MG - 1))
                else:
                    hi = z_hi[:, ring_slot(parity, g, HI_RING), :]
                    lo = z_lo[:, ring_slot(parity, g, LO_RING), :]
                    pe.wait_ge(hi_ready, rank(SPLIT, t, g))
                    for m in range(MG):
                        c = slice(m * COLS, (m + 1) * COLS)
                        nc.tensor.matmul(acc, w1_lo[:, SPLIT.index(g), m, :], hi[:, c], start=(g == 0 and m == 0), stop=False)
                        nc.tensor.matmul(acc, w1_hi[:, SPLIT.index(g), m, :], hi[:, c], start=False, stop=False)
                    if g in ON_POOL:
                        pe.wait_ge(lo_pool, rank(ON_POOL, t, g))
                    else:
                        pe.wait_ge(lo_dve, rank(ON_DVE, t, g))
                    for m in range(MG):
                        c = slice(m * COLS, (m + 1) * COLS)
                        last = nc.tensor.matmul(acc, w1_hi[:, SPLIT.index(g), m, :], lo[:, c], start=False,
                                                stop=(g == GROUPS - 1 and m == MG - 1))
                last.then_inc(mm_done, 1)

            pe.wait_ge(sel_ready, 1)
            pe.wait_ge(w0_lo_ready, 3)
            for t in range(2):
                for n in range(4):
                    l1_piece(t, n, t == 0)
                if t == 1:
                    for f in range(2):
                        x_form(0, f)
                l1_matmuls(t, t, 0, True)
                l1_matmuls(t, t, 1, True)
            pe.wait_ge(w1_lo_ready, 1)
            pe.wait_ge(small_in, 16 * (3 + len(FULL)))

            def tile(t, parity, more):
                pe.wait_ge(acc2_free, t + 1)
                for g in range(GROUPS):
                    if more and g < 4:
                        l1_piece(t + 2, g)
                    if g in FORMS_AT:
                        ahead, f = FORMS_AT[g]
                        if not (ahead and isinstance(t, int) and t == TILES - 1):
                            x_form(t + ahead, f)
                    group(t, g, parity)
                    if more and g in L1_AT:
                        l1_matmuls(t + 2, parity, L1_AT.index(g))

            every_tile(pe, tile)

            pe.wait_ge(tower_in, 32)
            pe.wait_ge(ctx_lo, 3)
            pe.wait_ge(z_ready, GROUPS * TILES)
            for half in range(2):
                c = slice(half * COLS, (half + 1) * COLS)
                pe.wait_ge(cur2_free, TILES - 31 if half == 0 else TILES + 1)
                for o in range(4):
                    n = slice(o * P, (o + 1) * P)
                    acc = ps[:, 4 * half + o, :]
                    nc.tensor.matmul(acc, wc_lhh[:, n], ctx_hhl[half], start=True, stop=False)
                    nc.tensor.matmul(acc, t1_w[:, 0, n], sums[:, 0, c], start=False, stop=False)
                    nc.tensor.matmul(acc, t1_w[:, 1, n], sums[:, 1, c], start=False, stop=True).then_inc(t_mm, 1)
            for half in range(2):
                pe.wait_ge(t_act, 4 * (half + 1))
                for o in range(2):
                    for k in range(4):
                        last = nc.tensor.matmul(ps[:, 2 * half + o, :], t2_w[:, k, o * P:(o + 1) * P],
                                                hidden[half][:, k * COLS:(k + 1) * COLS], start=(k == 0), stop=(k == 3))
                    last.then_inc(t_mm, 1)
            for half in range(2):
                pe.wait_ge(t_act, 8 + 2 * (half + 1))
                for k in range(2):
                    last = nc.tensor.matmul(ps[0:1, 4 + half, :], w3[:, k:k + 1], z1[:, 2 * half + k, :],
                                            start=(k == 0), stop=(k == 1))
                last.then_inc(t_mm, 1)


def selector_matrix():
    import numpy as np
    sel = np.zeros((PARTS, FIELDS, SELECTORS, P), np.float32)
    for row in range(P):
        j, low = row // 32, row % 32
        for f in range(FORMS):
            sel[:, H_CHUNK * f + row // M_CHUNK, f, row] = 1.0
        sel[:, low, FORMS, row] = 1.0
        for s in range(SHIFTS):
            sel[:, (low + S_CHUNK * s + j) % FIELDS, FORMS + 1 + s, row] = 1.0
        sel[:, (low + HALF) % FIELDS, FORMS + 1 + SHIFTS, row] = 1.0
    return sel.reshape(XROWS, SELECTORS * P)


def kernel(**inputs):
    import numpy as np
    import concourse.bacc as bacc
    from concourse.bass_utils import run_bass_kernel_spmd

    a = {name: np.ascontiguousarray(x) for name, x in inputs.items()}
    tables = [a[f"tbl_{f}"] for f in range(FIELDS)]
    w = a["L0_rec_filter_0"].reshape(FIELDS, FIELDS, N1)
    filt0 = np.zeros((P, SHIFTS + 1, N1), np.float32)
    filt0_t = np.zeros((P, SHIFTS + 1, N1), np.float32)
    for s in range(HALF + 1):
        for h in range(FIELDS if s < HALF else HALF):
            for copy in ((s % S_CHUNK,) if s < HALF else range(3)):
                row, chunk = copy * FIELDS + h, s // S_CHUNK
                filt0[row, chunk] = w[h, (h + s) % FIELDS]
                if s:
                    filt0_t[row, chunk] = w[(h + s) % FIELDS, h]
    v = a["L0_rec_filter_1"].reshape(FORMS, H_CHUNK, TURNS, M_CHUNK, N2)
    filt1 = np.zeros((H_CHUNK, M_CHUNK, GROUPS, MG, N2), np.float32)
    for n, g in enumerate(SPLIT + FULL):
        for j in range(H_CHUNK):
            for m in range(MG):
                filt1[j, :, n, m] = v[FORM_OF[g], j, (j + HALF_OF[g] * MG + m) % TURNS]
    filt1 = filt1.reshape(P, GROUPS * MG * N2)
    arrays = {
        "ctx_t": np.ascontiguousarray(a["dense_ctx"].T), "ids_in_dram": a["ids"],
        "w_top1": a["W_top1"], "b_top1": a["b_top1"], "w_top2": a["W_top2"], "b_top2": a["b_top2"],
        "w_top3": a["W_top3"], "filt0": filt0, "filt0_t": filt0_t, "filt1": filt1,
        "selectors": selector_matrix(),
    }
    for f in range(FIELDS):
        arrays[f"table_{f}"] = tables[f]
    nc = bacc.Bacc("TRN2", target_bir_lowering=False, num_devices=1)
    d = {n: nc.dram_tensor(n, x.shape, mybir.dt.from_np(x.dtype), kind="ExternalInput").ap() for n, x in arrays.items()}
    out = nc.dram_tensor("y_dram", (BATCH, 1), F32, kind="ExternalOutput").ap()
    build_dlrm(nc, d["ctx_t"], d["ids_in_dram"], [d[f"table_{f}"] for f in range(FIELDS)], d["w_top1"], d["b_top1"],
               d["w_top2"], d["b_top2"], d["w_top3"], d["filt0"], d["filt0_t"], d["filt1"], d["selectors"], out)
    r = run_bass_kernel_spmd(nc, [arrays], core_ids=[0])
    return r.results[0]["y_dram"]
```
